# Optimizing a Trainium2 kernel written in Bass

```python
import numpy as np
import jax
import jax.numpy as jnp

def _softmax(x, axis=-1):
    return jax.nn.softmax(x, axis=axis)

def _gelu(x):
    return jax.nn.gelu(x, approximate=True)

def _silu(x):
    return jax.nn.silu(x)

def _sigmoid(x):
    return jax.nn.sigmoid(x)

def _layernorm(x, axis=-1, eps=1e-05):
    m = jnp.mean(x, axis=axis, keepdims=True)
    v = jnp.var(x, axis=axis, keepdims=True)
    return (x - m) / jnp.sqrt(v + eps)

def _scatter_add(tgt, idx, src, axis=0):
    return tgt.at[idx].add(src)

def _segment_sum(src, seg, n):
    return jax.ops.segment_sum(src, seg, n)
kernel_name = 'mk_adaln_d1_jaxref_r8_5b86e5'

def setup_inputs(seed: int=0):
    np.random.seed(seed)
    _w = jnp.asarray

    def _L0_attn_setup():
        import jax, jax.numpy as jnp
        import numpy as np
        import math
        DK = 128
        key = jax.random.key(seed)
        k1, k2 = jax.random.split(key)
        x = jax.random.normal(k1, (4, 256, 128), dtype=jnp.float32)
        W = jax.random.normal(k2, (128, 3 * DK), dtype=jnp.float32) * (1.0 / math.sqrt(128))
        b = jnp.zeros((3 * DK,), dtype=jnp.float32)
        return {'x': x, 'W': W, 'b': b}
    _L0_attn_in = _L0_attn_setup()

    def _L0_ffn_setup():
        import jax, jax.numpy as jnp
        import numpy as np
        D = 128
        HQ = 16
        HKV = 4
        G = HQ // HKV
        K = 64
        V = 64
        E = 8
        TOPK = 2
        HID = 256
        CAP_FRAC = 0.125
        EPS = 1e-06

        def _rmsnorm(x, g):
            return x * jax.lax.rsqrt(jnp.mean(x * x, axis=-1, keepdims=True) + EPS) * g

        def _rotary_tables(t, dim):
            thetas = 10000.0 ** (-np.arange(0, dim, 2, dtype=np.float32) / dim)
            ticks = np.outer(np.arange(t, dtype=np.float32), thetas)
            ticks = np.tile(ticks, (1, 2))[None, :, None, :]
            return (jnp.asarray(np.cos(ticks)), jnp.asarray(np.sin(ticks)))

        def _neg_half(x):
            x1, x2 = jnp.split(x, 2, axis=-1)
            return jnp.concatenate([-x2, x1], axis=-1)

        def _attention(x, wq, wk, wv, wo):
            b, t, _ = x.shape
            q = (x @ wq).reshape(b, t, HQ, K)
            k = (x @ wk).reshape(b, t, HKV, K)
            v = (x @ wv).reshape(b, t, HKV, V)
            cos, sin = _rotary_tables(t, K)
            q = q * cos + _neg_half(q) * sin
            k = k * cos + _neg_half(k) * sin
            qg = q.reshape(b, t, G, HKV, K)
            scores = jnp.einsum('btghk,bThk->bghtT', qg, k)
            mask = jnp.tril(jnp.ones((t, t), bool))
            scores = jnp.where(mask, scores, -jnp.inf) / np.float32(np.sqrt(K))
            p = jax.nn.softmax(scores, axis=-1)
            out = jnp.einsum('bghtT,bThv->btghv', p, v).reshape(b, t, HQ * V)
            return out @ wo

        def _moe(x, router_w, router_b, w1, w2, w3):
            b, t, d = x.shape
            n = b * t
            xf = x.reshape(n, d)
            logits = xf @ router_w + router_b
            vals, idx = jax.lax.top_k(logits, TOPK)
            scores = jax.nn.softmax(vals, axis=-1)
            cap = int(np.floor(n * CAP_FRAC))
            oh = jax.nn.one_hot(idx, E, dtype=jnp.float32)
            pos = jnp.cumsum(jnp.cumsum(oh, axis=0), axis=1).astype(jnp.int32)
            emask = oh * (pos < cap)
            tmask = jnp.sum(emask, axis=-1)
            assign = jnp.einsum('tke,e->tk', emask, jnp.arange(E, dtype=jnp.float32)).astype(jnp.int32)
            m = jnp.max(assign, axis=-1)

            def ff(w1e, w2e, w3e):
                h = jax.nn.gelu(xf @ w2e * (xf @ w1e), approximate=False)
                return h @ w3e
            y_all = jax.vmap(ff)(w1, w2, w3)
            y = y_all[m, jnp.arange(n)]
            slot = jnp.where(tmask[..., None] > 0, y[:, None, :], xf[:, None, :])
            out = jnp.einsum('tkD,tk->tD', slot, scores)
            return out.reshape(b, t, d)
        key = jax.random.key(seed)
        ks = jax.random.split(key, 10)
        w = lambda k, shape: jax.random.normal(k, shape, jnp.float32) * 0.02
        return {'x': jax.random.normal(ks[0], (4, 64, D), jnp.float32), 'g1': jnp.ones((D,), jnp.float32), 'g2': jnp.ones((D,), jnp.float32), 'wq': w(ks[1], (D, HQ * K)), 'wk': w(ks[2], (D, HKV * K)), 'wv': w(ks[3], (D, HKV * V)), 'wo': w(ks[4], (HQ * V, D)), 'router_w': w(ks[5], (D, E)), 'router_b': jnp.zeros((E,), jnp.float32), 'w1': w(ks[6], (E, D, HID)), 'w2': w(ks[7], (E, D, HID)), 'w3': w(ks[8], (E, HID, D))}
    _L0_ffn_in = _L0_ffn_setup()
    _L0_c = _w((lambda *s: np.random.randn(*s).astype(np.float32) * 0.05)(16, 128))
    _L0_wmod = _w((lambda *s: np.random.randn(*s).astype(np.float32) * 0.05)(128, 6 * 128) * 128 ** (-0.5))
    _d = {'L0_attn_x': _L0_attn_in['x'], 'L0_attn_W': _L0_attn_in['W'], 'L0_attn_b': _L0_attn_in['b'], 'L0_ffn_g1': _L0_ffn_in['g1'], 'L0_ffn_g2': _L0_ffn_in['g2'], 'L0_ffn_wq': _L0_ffn_in['wq'], 'L0_ffn_wk': _L0_ffn_in['wk'], 'L0_ffn_wv': _L0_ffn_in['wv'], 'L0_ffn_wo': _L0_ffn_in['wo'], 'L0_ffn_router_w': _L0_ffn_in['router_w'], 'L0_ffn_router_b': _L0_ffn_in['router_b'], 'L0_ffn_w1': _L0_ffn_in['w1'], 'L0_ffn_w2': _L0_ffn_in['w2'], 'L0_ffn_w3': _L0_ffn_in['w3'], 'L0_c': _L0_c, 'L0_wmod': _L0_wmod}
    _x0 = _d['L0_attn_x']
    _d['L0_attn_x'] = jax.random.normal(jax.random.fold_in(jax.random.key(seed), 1), (16, 256, 128), dtype=_x0.dtype)
    del _x0
    return _d

def reference(L0_attn_x, L0_attn_W, L0_attn_b, L0_ffn_g1, L0_ffn_g2, L0_ffn_wq, L0_ffn_wk, L0_ffn_wv, L0_ffn_wo, L0_ffn_router_w, L0_ffn_router_b, L0_ffn_w1, L0_ffn_w2, L0_ffn_w3, L0_c, L0_wmod):

    def _L0_attn_ref(x, W, b):
        import jax, jax.numpy as jnp
        import numpy as np
        import math
        DK = 128
        qkv = jnp.einsum('btc,cd->btd', x, W) + b
        q, k, v = jnp.split(qkv, 3, axis=-1)
        scale = 1.0 / math.sqrt(DK)
        weights = jnp.einsum('btc,bTc->btT', q, k) * scale
        T = weights.shape[-1]
        mask = jnp.tril(jnp.ones((T, T), dtype=jnp.float32))
        logits = jnp.where(mask == 0, jnp.float32(-9000000000000000.0), weights)
        attention = jax.nn.softmax(logits, axis=-1)
        values = jnp.einsum('btT,bTc->btc', attention, v)
        return values

    def _L0_ffn_ref(x, g1, g2, wq, wk, wv, wo, router_w, router_b, w1, w2, w3):
        import jax, jax.numpy as jnp
        import numpy as np
        D = 128
        HQ = 16
        HKV = 4
        G = HQ // HKV
        K = 64
        V = 64
        E = 8
        TOPK = 2
        HID = 256
        CAP_FRAC = 0.125
        EPS = 1e-06

        def _rmsnorm(x, g):
            return x * jax.lax.rsqrt(jnp.mean(x * x, axis=-1, keepdims=True) + EPS) * g

        def _rotary_tables(t, dim):
            thetas = 10000.0 ** (-np.arange(0, dim, 2, dtype=np.float32) / dim)
            ticks = np.outer(np.arange(t, dtype=np.float32), thetas)
            ticks = np.tile(ticks, (1, 2))[None, :, None, :]
            return (jnp.asarray(np.cos(ticks)), jnp.asarray(np.sin(ticks)))

        def _neg_half(x):
            x1, x2 = jnp.split(x, 2, axis=-1)
            return jnp.concatenate([-x2, x1], axis=-1)

        def _attention(x, wq, wk, wv, wo):
            b, t, _ = x.shape
            q = (x @ wq).reshape(b, t, HQ, K)
            k = (x @ wk).reshape(b, t, HKV, K)
            v = (x @ wv).reshape(b, t, HKV, V)
            cos, sin = _rotary_tables(t, K)
            q = q * cos + _neg_half(q) * sin
            k = k * cos + _neg_half(k) * sin
            qg = q.reshape(b, t, G, HKV, K)
            scores = jnp.einsum('btghk,bThk->bghtT', qg, k)
            mask = jnp.tril(jnp.ones((t, t), bool))
            scores = jnp.where(mask, scores, -jnp.inf) / np.float32(np.sqrt(K))
            p = jax.nn.softmax(scores, axis=-1)
            out = jnp.einsum('bghtT,bThv->btghv', p, v).reshape(b, t, HQ * V)
            return out @ wo

        def _moe(x, router_w, router_b, w1, w2, w3):
            b, t, d = x.shape
            n = b * t
            xf = x.reshape(n, d)
            logits = xf @ router_w + router_b
            vals, idx = jax.lax.top_k(logits, TOPK)
            scores = jax.nn.softmax(vals, axis=-1)
            cap = int(np.floor(n * CAP_FRAC))
            oh = jax.nn.one_hot(idx, E, dtype=jnp.float32)
            pos = jnp.cumsum(jnp.cumsum(oh, axis=0), axis=1).astype(jnp.int32)
            emask = oh * (pos < cap)
            tmask = jnp.sum(emask, axis=-1)
            assign = jnp.einsum('tke,e->tk', emask, jnp.arange(E, dtype=jnp.float32)).astype(jnp.int32)
            m = jnp.max(assign, axis=-1)

            def ff(w1e, w2e, w3e):
                h = jax.nn.gelu(xf @ w2e * (xf @ w1e), approximate=False)
                return h @ w3e
            y_all = jax.vmap(ff)(w1, w2, w3)
            y = y_all[m, jnp.arange(n)]
            slot = jnp.where(tmask[..., None] > 0, y[:, None, :], xf[:, None, :])
            out = jnp.einsum('tkD,tk->tD', slot, scores)
            return out.reshape(b, t, d)
        h = x + _attention(_rmsnorm(x, g1), wq, wk, wv, wo)
        return h + _moe(_rmsnorm(h, g2), router_w, router_b, w1, w2, w3)
    x = L0_attn_x
    mod = (_silu(L0_c) @ L0_wmod).reshape(L0_c.shape[0], 6, 1, -1)
    sa, ca, ga, sb, cb, gb = (mod[:, 0], mod[:, 1], mod[:, 2], mod[:, 3], mod[:, 4], mod[:, 5])
    ga = (2 * (ga >= 0) - 1) * jnp.maximum(jnp.abs(ga), 0.25)
    gb = (2 * (gb >= 0) - 1) * jnp.maximum(jnp.abs(gb), 0.25)
    h = _layernorm(x, axis=-1) * (1 + ca) + sa
    x = x + ga * _L0_attn_ref(h, L0_attn_W, L0_attn_b)
    h = _layernorm(x, axis=-1) * (1 + cb) + sb
    x = x + gb * _L0_ffn_ref(h, L0_ffn_g1, L0_ffn_g2, L0_ffn_wq, L0_ffn_wk, L0_ffn_wv, L0_ffn_wo, L0_ffn_router_w, L0_ffn_router_b, L0_ffn_w1, L0_ffn_w2, L0_ffn_w3)
    return x

_drawn_inputs = setup_inputs


def setup_inputs(seed=0):
    import zlib

    import numpy as np

    out = dict(_drawn_inputs(seed))
    spreads = {'L0_attn_b': (0.0, 0.281),
     'L0_ffn_g1': (1.0, 0.6),
     'L0_ffn_g2': (1.0, 0.2),
     'L0_ffn_router_b': (0.0, 0.1)}
    factors = {'L0_ffn_wq': 8.0,
     'L0_ffn_wk': 8.0,
     'L0_ffn_wv': 3.639,
     'L0_ffn_wo': 3.895,
     'L0_ffn_w1': 8.0,
     'L0_ffn_w2': 8.0,
     'L0_ffn_w3': 8.0}
    for name, (base, spread) in spreads.items():
        noise = np.random.default_rng([zlib.crc32(name.encode()), seed]).standard_normal(out[name].shape)
        drawn = base * np.exp(spread * noise) if base else spread * noise
        out[name] = jnp.asarray(drawn.astype(out[name].dtype))
    for name, factor in factors.items():
        out[name] = (out[name] * factor).astype(out[name].dtype)
    return out
```

```python
from contextlib import ExitStack

import numpy as np

import concourse.bass as bass
from concourse import mybir

ALU = mybir.AluOpType
ACT = mybir.ActivationFunctionType
F32 = mybir.dt.float32
BF16 = mybir.dt.bfloat16
U32 = mybir.dt.uint32
I32 = mybir.dt.int32
AX_X = mybir.AxisListType.X

P = 128
NBATCH, T, D = 16, 256, 128
NT = T // P
HQ, HKV, K = 16, 4, 64
QKV = (HQ + 2 * HKV) * K
NCH = HQ * K // P
E, HID = 8, 256
NTOK = NBATCH * T
CAP = NTOK // 8
ROWS = 2 * CAP
DUMP = E * ROWS
NBLK = 40
MASKED = -1e30

C_IOTA8 = 0
C_DUMP = 8
C_THR = C_DUMP + NBATCH * NT
C_LOWER = C_THR + 64
C_BLK = C_LOWER + 64
C_HALF = C_BLK + NBLK
C_END = C_HALF + 2

ZCOLS = 1024
ZEROED = 16 * 4
SETUP_SILU, SETUP_SCT, SETUP_MOD, SETUP_ALL = 3, 4, 8, 9
STATS_LINKS, FRONT_LINKS, ATTN_LINKS, TAIL_LINKS = 1, 5, 8, 24

QUADS = [(i, g) for g in range(4) for i in range(NT)]

SLOTS = [
    (("f_stats", "t_ot00"), ("t_ot10", "f_xnT"), ("f_qk",)),
    (("t_ot01", "f_va"), ("t_ot11", "f_sa"), ("f_ea",)),
    (("f_ta",), ("t_wo", "f_pva"), ("f_ln2",)),
    (("t_sq", "f_rms"), ("f_xrT",), ("f_p0k",)),
    (("t_xf", "f_p0a"), ("t_xfT", "f_p0b"), ("f_p1k", "t_logits")),
    (("f_p1a", "f_k0T"), ("f_p1b",), ("f_q00T", "t_cum")),
    (("f_q01T", "f_k1T"), ("f_q10T", "t_rank"), ("f_q11T",)),
    ((), ("t_base",), ()),
]
NO_BANK = ("f_stats", "f_ea", "f_ln2", "f_rms", "t_sq", "t_xf", "t_base")
FRONT = [s for slot in SLOTS for place in slot for s in place if s[0] == "f"]
TAIL = [s for slot in SLOTS for place in slot for s in place if s[0] == "t"]


def shared_order(front, tail):
    out = []
    for u, places in enumerate(SLOTS):
        for k, place in enumerate(places):
            if k == 2:
                out.append(f"pv{u}")
            out += [s for s in place if s not in NO_BANK and (front if s[0] == "f" else tail)]
    return out


MIDDLE_ORDER = shared_order(True, True)
BANK = {s: n % 2 for n, s in enumerate(MIDDLE_ORDER)}
ORDERS = {"prologue": [s for s in FRONT if s not in NO_BANK], "first": shared_order(True, False), "middle": MIDDLE_ORDER,
          "last": shared_order(False, True), "end": [s for s in TAIL if s not in NO_BANK]}


def uses_before(stage, part, b):
    bank = BANK[stage]
    n = {p: sum(BANK[s] == bank for s in o) for p, o in ORDERS.items()}
    order = ORDERS[part]
    here = sum(BANK[s] == bank for s in order[:order.index(stage)])
    if part == "prologue":
        return here
    if part == "first":
        return n["prologue"] + here
    if part == "middle":
        return (b - 1) * n["middle"] + (n["prologue"] + n["first"] + here)
    before_last = n["prologue"] + n["first"] + (NBATCH - 2) * n["middle"]
    return before_last + (here if part == "last" else n["last"] + here)


def span(start, size):
    return slice(start, start + size) if isinstance(start, int) else bass.ds(start, size)


def wait(eng, sem, value):
    if isinstance(value, int) and value <= 0:
        return
    eng.wait_ge(sem, value)


def wait_alone(eng, sem, value, held):
    if not isinstance(value, int):
        value = eng.snap(eng.to_reg(value))
        eng.wait_ge(*held)
    eng.wait_ge(sem, value)


def parts(eng, body):
    body("prologue", -1, 1)
    body("first", 0, 0)
    with eng.Fori(1, NBATCH - 2, 2) as b:
        body("middle", b, 1)
        body("middle", b + 1, 0)
    body("last", NBATCH - 1, 1)
    body("end", NBATCH, 0)


def stages_of(part):
    if part == "prologue":
        for s in FRONT:
            yield "stage", s
        yield "scores", 0
        yield "scores", 1
        return
    if part == "end":
        for s in TAIL:
            yield "stage", s
        return
    for u, places in enumerate(SLOTS):
        yield "transpose", u
        for k, place in enumerate(places):
            if k == 1 and not (part == "last" and u >= 6):
                yield "scores", u + 2
            if k == 2:
                yield "values", u
            for s in place:
                if s[0] == "f" and part == "last":
                    continue
                if s[0] == "t" and part == "first":
                    continue
                yield "stage", s


def adaln_layer(nc, x, W, bias, g1, g2, wq, wk, wv, wo, router_w, router_b, w1, w2, w3, c, wmod,
                k_ident, k_mask, k_upper, k_rope, k_small, out):
    ctx = ExitStack()
    with ctx:
        def sb(name, shape, dt=F32):
            return ctx.enter_context(nc.sbuf_tensor(name, shape, dt))

        def pb(name, shape):
            return ctx.enter_context(nc.psum_tensor(name, shape, F32))

        def sem(name):
            return ctx.enter_context(nc.semaphore(name))

        xs_dram = nc.dram_tensor("expert_rows", (DUMP + NTOK, D), F32, kind="Internal").ap()
        ys_dram = nc.dram_tensor("expert_results", (DUMP + NBLK * P, D), F32, kind="Internal").ap()
        mod_dram = nc.dram_tensor("modulation_rows", (NBATCH, 4 * D), F32, kind="Internal").ap()

        ident = sb("ident", [P, P])
        stage_f32 = sb("stage_f32", [P, 2, P])
        mask_bf = sb("mask_bf", [P, P], BF16)
        ident_bf = sb("ident_bf", [P, P], BF16)
        upper_bf = sb("upper_bf", [P, P], BF16)
        ones_bf = sb("ones_bf", [P, P], BF16)
        rope = sb("rope", [P, 4, NT, K])
        small = sb("small", [P, C_END])
        wa_sb = sb("wa_sb", [P, 3 * D])
        wqkv_sb = sb("wqkv_sb", [P, QKV])
        wo_sb = sb("wo_sb", [P, NCH, D])
        wmod_sb = sb("wmod_sb", [P, 6 * D])
        rw_sb = sb("rw_sb", [P, E])
        w12_sb = sb("w12_sb", [P, E, 2 * HID])
        w3_sb = sb("w3_sb", [P, E, 2, D])
        qk_bias = sb("qk_bias", [P, 2])
        g1_col = sb("g1_col", [P, 1])
        bv_bc = sb("bv_bc", [P, D])
        g2_bc = sb("g2_bc", [P, D])
        rb_bc = sb("rb_bc", [P, E])

        c_sb = sb("c_sb", [NBATCH, D])
        c_tmp = sb("c_tmp", [NBATCH, 2, D])
        scT = sb("scT", [P, NBATCH])
        modT = sb("modT", [P, 2, NBATCH])
        mod_rows = sb("mod_rows", [NBATCH, 4, D])
        mod_sign = sb("mod_sign", [NBATCH, 2, D])
        mod_mag = sb("mod_mag", [NBATCH, 2, D])
        mod_all = sb("mod_all", [P, NBATCH, 4, D])
        GA, SB, CB, GB = range(4)

        x_in = [sb(f"x_in{k}", [P, NT, D]) for k in range(2)]
        stats = sb("stats", [P, NT, 6])
        mv = sb("mv", [P, NT, 2])
        rstd = sb("rstd", [P, NT])
        var_eps = sb("var_eps", [P, NT])
        xn = sb("xn", [P, NT, D])
        hT = sb("hT", [P, T])
        qkA = sb("qkA", [P, 2, T])
        vA = sb("vA", [P, NT, D])
        biasA = sb("biasA", [P, NT])
        sumA = sb("sumA", [P, NT])
        rsumA = sb("rsumA", [P, NT])
        probsA = sb("probsA", [P, 3 * P])
        probsAT = sb("probsAT", [P, 3 * P])
        attA = sb("attA", [P, NT, D])
        stats2 = sb("stats2", [P, NT, 6])
        mv2 = sb("mv2", [P, NT, 2])
        rstd2 = sb("rstd2", [P, NT])
        var2_eps = sb("var2_eps", [P, NT])
        xn2 = sb("xn2", [P, NT, D])
        h2 = [sb(f"h2_{k}", [P, NT, D]) for k in range(2)]
        squares = sb("squares", [P, NT, D])
        ms2 = sb("ms2", [P, NT])
        ms2_eps = sb("ms2_eps", [P, NT])
        rms2 = sb("rms2", [P, NT])
        xr = sb("xr", [P, NT, D])
        xrT = sb("xrT", [P, T])
        rope_cos = [sb(f"rope_cos{k}", [P, 512]) for k in range(2)]
        rope_sin = [sb(f"rope_sin{k}", [P, 512]) for k in range(2)]
        qtok = sb("qtok", [P, NT, HQ + HKV, K])
        qT = [sb(f"qT{k}", [P, NCH, T]) for k in range(2)]
        kT = [sb(f"kT{k}", [P, HKV // 2, T]) for k in range(2)]
        v1 = [sb(f"v1_{k}", [P, NT, HKV, K + 1]) for k in range(2)]

        negmax = [sb(f"negmax{k}", [P, 2, 2]) for k in range(2)]
        probs = [sb(f"probs{k}", [P, HKV, T]) for k in range(2)]
        probsT = [sb(f"probsT{k}", [P, 2 * HKV, P]) for k in range(2)]
        rden = sb("rden", [P, HKV])
        attn = sb("attn", [P, NT, HQ * K])

        attnT = sb("attnT", [P, NCH, T])
        h = sb("h", [P, NT, D])
        squares3 = sb("squares3", [P, NT, D])
        ms3 = sb("ms3", [P, NT])
        ms3_eps = sb("ms3_eps", [P, NT])
        rms3 = sb("rms3", [P, NT])
        xf = sb("xf", [P, NT, D])
        xfT = sb("xfT", [P, T])
        logits = sb("logits", [P, NT, E])
        top8 = sb("top8", [P, NT, E])
        idx8 = sb("idx8", [P, NT, E], U32)
        idxf = sb("idxf", [P, NT, 2])
        gap = sb("gap", [P, NT])
        gap_exp = sb("gap_exp", [P, NT])
        gap_den = sb("gap_den", [P, NT])
        score = sb("score", [P, NT, 2])
        picked = sb("picked", [P, NT, 2, E])
        picked_bf = sb("picked_bf", [P, NT, 2, E], BF16)
        seen_bf = sb("seen_bf", [P, 2, E], BF16)
        kept = sb("kept", [P, NT, 2, E])
        kept_id = sb("kept_id", [P, NT, 2, E])
        kept_any = sb("kept_any", [P, NT, 2])
        kept_expert = sb("kept_expert", [P, NT, 2])
        has = sb("has", [P, NT])
        expert = sb("expert", [P, NT])
        kept_score = sb("kept_score", [P, NT, 2])
        score_sum = sb("score_sum", [P, NT])
        drop_score = sb("drop_score", [P, NT])
        mine = sb("mine", [P, NT, E])
        mine_bf = sb("mine_bf", [P, NT, E], BF16)
        filled_bf = sb("filled_bf", [P, E], BF16)
        rank_of = sb("rank_of", [P, NT, E])
        rank = sb("rank", [P, NT])
        row = sb("row", [P, NT])
        dump_row = sb("dump_row", [P, NT])
        gather_row = sb("gather_row", [P, NT])
        scatter_idx = sb("scatter_idx", [P, NT], U32)
        gather_all = sb("gather_all", [P, NBATCH * NT], U32)
        score_all = sb("score_all", [P, NBATCH * NT])
        base_all = sb("base_all", [P, NBATCH * NT, D])
        base_tmp = sb("base_tmp", [P, NT, D])

        xb = [qT[0][:, 0, k * P:(k + 1) * P] for k in range(2)]
        xbT = [qT[0][:, 1, k * P:(k + 1) * P] for k in range(2)]
        up = [qT[0][:, 2 + k, :] for k in range(2)]
        prod = [qT[0][:, 4 + k, :] for k in range(2)]
        hid = [qT[0][:, 6 + k, :] for k in range(2)]
        hidT = [qT[1][:, k, :] for k in range(2)]
        yb = [qT[1][:, 2, k * P:(k + 1) * P] for k in range(2)]
        yg = [qT[1][:, 3 + k, :].rearrange("p (i d) -> p i d", i=NT) for k in range(2)]
        yo = [qT[1][:, 5 + k, :].rearrange("p (i d) -> p i d", i=NT) for k in range(2)]
        gather_pair = [sb(f"gather_pair{k}", [P, NT], U32) for k in range(2)]
        zeros = sb("zeros", [P, ZCOLS])
        blk_need = sb("blk_need", [P, E, E])
        blk_cnt = sb("blk_cnt", [P, E])
        blk_cum = sb("blk_cum", [P, E])
        blk_past = sb("blk_past", [P, NBLK, E])
        blk_pastn = sb("blk_pastn", [P, NBLK, E])
        blk_f = sb("blk_f", [P, 8, NBLK])
        blk_tab = sb("blk_tab", [P, 3, NBLK], I32)

        scores = [[pb(f"scores{k}{half}", [P, 2, T]) for half in range(2)] for k in range(2)]
        tposed = [pb(f"tposed{k}", [P, 512]) for k in range(2)]
        shared = [pb(f"shared{k}", [P, 512]) for k in range(2)]

        s_const = sem("const_loaded")
        s_w = sem("weights_loaded")
        s_moew = sem("expert_weights_loaded")
        s_modout = sem("mod_rows_stored")
        s_modin = sem("mod_all_loaded")
        s_x = [sem(f"x_loaded{k}") for k in range(2)]
        s_zero = sem("expert_rows_zeroed")
        s_zeros = sem("zero_source_ready")
        s_setup_act = sem("setup_act")
        s_setup_dve = sem("setup_dve")
        s_setup_pe = sem("setup_pe")
        s_full = [sem(f"shared_full{k}") for k in range(2)]
        s_free = [sem(f"shared_free{k}") for k in range(2)]
        s_scores = sem("scores_full")
        s_negmax = sem("negmax_ready")
        s_probs = sem("probs_ready")
        s_tfull = sem("tposed_full")
        s_tfree = sem("tposed_free")
        s_v1 = sem("v1_ready")
        s_var = sem("var_ready")
        s_rstd = sem("rstd_ready")
        s_xn = sem("xn_ready")
        s_biasA = sem("biasA_ready")
        s_var2 = sem("var2_ready")
        s_rstd2 = sem("rstd2_ready")
        s_x2 = sem("x2_done")
        s_h2 = sem("h2_ready")
        s_ms2 = sem("ms2_ready")
        s_rms2 = sem("rms2_ready")
        s_xr = sem("xr_ready")
        s_roped = sem("roped")
        s_ms3 = sem("ms3_ready")
        s_rms3 = sem("rms3_ready")
        s_xf = sem("xf_ready")
        s_gap = sem("gap_ready")
        s_gexp = sem("gap_exp_ready")
        s_picked = sem("picked_ready")
        s_mine = sem("mine_ready")
        s_sidx = sem("scatter_idx_ready")
        s_scat = sem("rows_scattered")
        s_dfront = sem("dve_front_chain")
        s_dattn = sem("dve_attn_chain")
        s_dtail = sem("dve_tail_chain")
        s_vareps, s_var2eps = sem("var_eps_ready"), sem("var2_eps_ready")
        s_ms2eps, s_ms3eps = sem("ms2_eps_ready"), sem("ms3_eps_ready")
        s_filled = sem("filled_ready")
        s_dstats = sem("dve_stats_chain")
        s_dend = sem("dve_end_chain")
        s_gidx = sem("gather_idx_ready")
        s_tab = sem("block_table_ready")
        s_total = sem("totals_ready")
        s_xb = [sem(f"xb_loaded{k}") for k in range(2)]
        s_xbTp = sem("xb_transposed")
        s_xbT = sem("xbT_ready")
        s_up = sem("up_products")
        s_upc = sem("up_copied")
        s_prod = sem("prod_ready")
        s_hid = sem("hid_ready")
        s_hTp = sem("hid_transposed")
        s_hT = sem("hidT_ready")
        s_yp = sem("y_product")
        s_yb = sem("yb_ready")
        s_ys = [sem(f"y_stored{k}") for k in range(2)]
        s_yg = [sem(f"y_gathered{k}") for k in range(2)]
        s_scaled = sem("y_scaled")
        s_yo = sem("yo_ready")
        s_out = [sem(f"out_stored{k}") for k in range(2)]

        CONSTS = (s_const, 6 * 16)
        iota8 = small[:, C_IOTA8:C_IOTA8 + E]
        block = ctx.enter_context(nc.Block())

        @block.sync
        def _(sp):
            def load_x(n, k):
                sp.dma_start(x_in[k][:, :, :], x[n, :, :].rearrange("(i p) d -> p i d", p=P)
                             if isinstance(n, int) else
                             x[bass.ds(n, 1), :, :].rearrange("b (i p) d -> p (b i) d", p=P)).then_inc(s_x[k], 16)

            load_x(0, 0)
            sp.dma_start(c_sb[:, :], c).then_inc(s_const, 16)
            sp.dma_start(ident[:, :], k_ident).then_inc(s_const, 16)
            sp.dma_start(wmod_sb[:, :], wmod).then_inc(s_const, 16)
            sp.dma_start(stage_f32[:, 0, :], k_mask).then_inc(s_const, 16)
            sp.dma_start(stage_f32[:, 1, :], k_upper).then_inc(s_const, 16)
            sp.dma_start(small[:, :], k_small).then_inc(s_const, 16)
            sp.dma_start(wa_sb[:, :], W).then_inc(s_w, 16)
            sp.dma_start(qk_bias[:, :], bias[0:2 * D].rearrange("(j p) -> p j", p=P),
                         allow_slow_non_contiguous=True).then_inc(s_w, 16)
            sp.dma_start(bv_bc[:, :], bias[2 * D:3 * D].rearrange("(a d) -> a d", a=1).to_broadcast([P, D])
                         ).then_inc(s_w, 16)
            sp.dma_start(g1_col[:, :], g1.rearrange("(p a) -> p a", a=1)).then_inc(s_w, 16)
            sp.dma_start(g2_bc[:, :], g2.rearrange("(a d) -> a d", a=1).to_broadcast([P, D])).then_inc(s_w, 16)
            sp.dma_start(rb_bc[:, :], router_b.rearrange("(a d) -> a d", a=1).to_broadcast([P, E])
                         ).then_inc(s_w, 16)
            sp.dma_start(rw_sb[:, :], router_w).then_inc(s_w, 16)
            sp.dma_start(rope[:, :, :, :], k_rope).then_inc(s_w, 16)
            sp.dma_start(wqkv_sb[:, 0:HQ * K], wq).then_inc(s_w, 16)
            sp.dma_start(wqkv_sb[:, HQ * K:(HQ + HKV) * K], wk).then_inc(s_w, 16)
            sp.dma_start(wqkv_sb[:, (HQ + HKV) * K:], wv).then_inc(s_w, 16)
            sp.dma_start(wo_sb[:, :, :], wo.rearrange("(c p) d -> p c d", p=P)).then_inc(s_w, 16)
            load_x(1, 1)
            sp.wait_ge(s_setup_dve, SETUP_MOD)
            sp.dma_start(mod_dram, mod_rows[:, :, :].rearrange("b j d -> b (j d)")).then_inc(s_modout, 16)
            sp.wait_ge(s_modout, 16)
            for q in range(4):
                n = NBATCH // 4
                sp.dma_start(mod_all[:, q * n:(q + 1) * n, :, :],
                             mod_dram[q * n:(q + 1) * n, :].rearrange("(a b) j -> a (b j)", a=1)
                             .to_broadcast([P, n * 4 * D])).then_inc(s_modin, 16)
            sp.wait_ge(s_zeros, 1)
            per = P * ZCOLS // D
            for rows in (xs_dram, ys_dram):
                for q in range(2):
                    half = rows[q * DUMP // 2:(q + 1) * DUMP // 2, :]
                    n = DUMP // 2 // per
                    sp.dma_start(half.rearrange("(n p r) d -> p n (r d)", n=n, p=P),
                                 zeros[:, :].unsqueeze(1).to_broadcast([P, n, ZCOLS])).then_inc(s_zero, 16)
            for e in range(E):
                sp.dma_start(w12_sb[:, e, 0:HID], w1[e]).then_inc(s_moew, 16)
                sp.dma_start(w12_sb[:, e, HID:], w2[e]).then_inc(s_moew, 16)
                sp.dma_start(w3_sb[:, e, :, :], w3[e].rearrange("(c p) d -> p c d", p=P)).then_inc(s_moew, 16)
            with sp.Fori(2, NBATCH - 1, 2) as n:
                sp.wait_ge(s_x2, n - 1)
                load_x(n, 0)
                sp.wait_ge(s_x2, n)
                load_x(n + 1, 1)

            sp.wait_ge(s_tab, 1)
            sp.wait_ge(s_scat, 16 * NBATCH * NT)

            def load_block(j, k):
                r = sp.value_load(blk_tab[0:1, 1, bass.ds(j, 1)], min_val=0, max_val=DUMP - P)
                sp.dma_start(xb[k], xs_dram[bass.ds(r, P), :]).then_inc(s_xb[k], 16)

            def store_block(j, k):
                r = sp.value_load(blk_tab[0:1, 2, bass.ds(j, 1)], min_val=0, max_val=DUMP + (NBLK - 1) * P)
                sp.wait_ge(s_yb, j + 1)
                sp.dma_start(ys_dram[bass.ds(r, P), :], yb[k]).then_inc(s_ys[k], 16)

            load_block(0, 0)
            load_block(1, 1)
            for j in range(2, 4):
                sp.wait_ge(s_xbTp, j - 1)
                load_block(j, j % 2)
            with sp.Fori(0, NBLK - 5, 2) as j:
                for k in range(2):
                    sp.wait_ge(s_xbTp, j + (k + 3))
                    load_block(j + (k + 4), k)
                    store_block(j + k, k)
            for j in range(NBLK - 4, NBLK):
                store_block(j, j % 2)

            def store_out(b, k):
                sp.wait_ge(s_yo, b + 1)
                sp.dma_start(out[bass.ds(b, 1), :, :].rearrange("b (i p) d -> p (b i) d", p=P),
                             yo[k]).then_inc(s_out[k], 16)

            with sp.Fori(0, NBATCH - 1, 2) as b:
                store_out(b, 0)
                store_out(b + 1, 1)
            for k in range(2):
                sp.wait_ge(s_out[k], 16 * NBATCH // 2)

        @block.tensor
        def _(pe):
            mm, tr = nc.tensor.matmul, nc.tensor.transpose

            pe.wait_ge(s_const, 6 * 16)
            pe.wait_ge(s_setup_dve, SETUP_SILU)
            tr(shared[0][:, 0:NBATCH], c_tmp[:, 1, :], ident[0:NBATCH, 0:NBATCH]).then_inc(s_setup_pe, 1)
            pe.wait_ge(s_setup_dve, SETUP_SCT)
            mm(shared[1][0:NBATCH, :], scT[:, :], wmod_sb[:, 2 * D:6 * D], start=True, stop=True
               ).then_inc(s_setup_pe, 1)
            for j in range(2):
                last = mm(shared[0][:, j * NBATCH:(j + 1) * NBATCH], wmod_sb[:, j * D:(j + 1) * D], scT[:, :],
                          start=True, stop=True)
            last.then_inc(s_setup_pe, 1)
            pe.wait_ge(s_setup_dve, SETUP_ALL)
            pe.wait_ge(s_w, 12 * 16)

            def evacuated(stages, part, b, into=None):
                for bank in range(2):
                    of_bank = [s for s in stages if BANK[s] == bank]
                    if of_bank and (into is None or bank != BANK[into]):
                        pe.wait_ge(s_free[bank], uses_before(of_bank[-1], part, b) + 1)

            def scores_of(u, n, k):
                i, g = QUADS[u]
                wait(pe, s_probs, 8 * n + (u - 1))
                nk = (i + 1) * P
                banks = scores[u % 2]
                for half in range(2):
                    mm(banks[half][:, :, i * P:(i + 1) * P], ident_bf[:, :],
                       mask_bf[:, :].unsqueeze(1).to_broadcast([P, 2, P]), start=True, stop=False,
                       skip_group_check=True)
                for kv in range(HKV):
                    half, rows = kv % 2, slice(K * (kv % 2), K * (kv % 2) + K)
                    last = mm(banks[half][:, kv // 2, 0:nk], qT[k][rows, 2 * g + kv // 2, i * P:(i + 1) * P],
                              kT[k][rows, kv // 2, 0:nk], start=False, stop=True, skip_group_check=True)
                last.then_inc(s_scores, 1)

            def body(part, b, k):
                n = b + 1
                nk = 1 - k
                before = {"prologue": None, "first": ("prologue", -1), "middle": ("middle", b - 1),
                          "last": ("middle", b - 1), "end": ("last", b - 1)}[part]
                t_used = 0
                for kind, what in stages_of(part):
                    if kind == "scores":
                        u = what
                        if u in (8, 9) or part == "prologue":
                            u %= 8
                            evacuated(("f_k0T", "f_q00T") if u == 0 else ("f_k1T", "f_q10T"), part, b)
                            scores_of(u, n, nk)
                        else:
                            if u == 2:
                                evacuated(["f_q11T"], *before)
                            scores_of(u, b, k)
                        continue
                    if kind == "transpose":
                        u = what
                        i, g = QUADS[u]
                        pe.wait_ge(s_probs, 8 * b + (u + 1))
                        blocks = [(kv, kt) for kv in range(HKV) for kt in range(i + 1)]
                        for at in range(0, len(blocks), 4):
                            wait(pe, s_tfree, 12 * b + (t_used - 1))
                            for m, (kv, kt) in enumerate(blocks[at:at + 4]):
                                last = tr(tposed[t_used % 2][:, m * P:(m + 1) * P],
                                          probs[u % 2][:, kv, kt * P:(kt + 1) * P], ident[:, :])
                            last.then_inc(s_tfull, 1)
                            t_used += 1
                        continue
                    stage = f"pv{what}" if kind == "values" else what
                    if stage in NO_BANK:
                        continue
                    bank = shared[BANK[stage]]
                    wait(pe, s_free[BANK[stage]], uses_before(stage, part, b))
                    if kind == "values":
                        i, g = QUADS[what]
                        pe.wait_ge(s_tfree, 12 * b + t_used)
                        if what < 2:
                            pe.wait_ge(s_v1, 2 * b + (what + 1))
                        for kv in range(HKV):
                            for kt in range(i + 1):
                                last = mm(bank[:, kv * (K + 1):(kv + 1) * (K + 1)],
                                          probsT[what % 2][:, kv * (i + 1) + kt, :], v1[k][:, kt, kv, :],
                                          start=kt == 0, stop=kt == i)
                    elif stage == "f_xnT":
                        pe.wait_ge(s_xn, n + 1)
                        for i in range(NT):
                            last = tr(bank[:, i * P:(i + 1) * P], xn[:, i, :], ident[:, :])
                    elif stage == "f_qk":
                        evacuated(["f_xnT"], part, b, into=stage)
                        for j in range(2):
                            last = mm(bank[:, j * T:(j + 1) * T], wa_sb[:, j * D:(j + 1) * D], hT[:, :],
                                      start=True, stop=True)
                    elif stage == "f_va":
                        for i in range(NT):
                            last = mm(bank[:, i * P:(i + 1) * P], hT[:, i * P:(i + 1) * P],
                                      wa_sb[:, 2 * D:3 * D], start=True, stop=True)
                    elif stage == "f_sa":
                        evacuated(["f_qk"], part, b, into=stage)
                        for i in range(NT):
                            mm(bank[:, 2 * i * P:(2 * i + 1) * P], ident_bf[:, :], mask_bf[:, :],
                               start=True, stop=False, skip_group_check=True)
                            last = mm(bank[:, i * P:(2 * i + 1) * P], qkA[:, 0, i * P:(i + 1) * P],
                                      qkA[:, 1, 0:(i + 1) * P], start=False, stop=True, skip_group_check=True)
                    elif stage == "f_ta":
                        evacuated(["f_sa"], part, b, into=stage)
                        for j in range(3):
                            last = tr(bank[:, j * P:(j + 1) * P], probsA[:, j * P:(j + 1) * P], ident[:, :])
                    elif stage == "f_pva":
                        evacuated(["f_va", "f_ta"], part, b, into=stage)
                        mm(bank[:, 0:P], probsAT[:, 0:P], vA[:, 0, :], start=True, stop=True)
                        mm(bank[:, P:2 * P], probsAT[:, P:2 * P], vA[:, 0, :], start=True, stop=False)
                        last = mm(bank[:, P:2 * P], probsAT[:, 2 * P:3 * P], vA[:, 1, :], start=False, stop=True)
                    elif stage == "f_xrT":
                        pe.wait_ge(s_xr, n + 1)
                        for i in range(NT):
                            last = tr(bank[:, i * P:(i + 1) * P], xr[:, i, :], ident[:, :])
                    elif stage.startswith("f_p"):
                        evacuated(["f_xrT"], part, b, into=stage)
                        i, j = int(stage[3]), "abk".index(stage[4])
                        last = mm(bank[:, :], xrT[:, i * P:(i + 1) * P], wqkv_sb[:, j * 512:(j + 1) * 512],
                                  start=True, stop=True)
                    elif stage.startswith("f_k") or stage.startswith("f_q"):
                        i = int(stage[3])
                        first, count = (HQ // 2, 2) if stage[2] == "k" else (4 * int(stage[4]), 4)
                        done = 1 if stage[2] == "k" else 2 + int(stage[4])
                        pe.wait_ge(s_roped, 6 * n + (3 * i + done))
                        for m in range(count):
                            last = tr(bank[:, m * P:(m + 1) * P],
                                      qtok[:, i, 2 * (first + m):2 * (first + m) + 2, :]
                                      .rearrange("p h d -> p (h d)"), ident[:, :])
                    elif stage.startswith("t_ot"):
                        i, part4 = int(stage[4]), int(stage[5])
                        evacuated(["pv7"], *before, into=stage)
                        for m in range(4):
                            ch = 4 * part4 + m
                            last = tr(bank[:, m * P:(m + 1) * P], attn[:, i, ch * P:(ch + 1) * P], ident[:, :])
                    elif stage == "t_wo":
                        evacuated(["t_ot00", "t_ot10", "t_ot01", "t_ot11"], part, b, into=stage)
                        for i in range(NT):
                            for ch in range(NCH):
                                last = mm(bank[:, i * P:(i + 1) * P], attnT[:, ch, i * P:(i + 1) * P],
                                          wo_sb[:, ch, :], start=ch == 0, stop=ch == NCH - 1)
                    elif stage == "t_xfT":
                        pe.wait_ge(s_xf, b)
                        for i in range(NT):
                            last = tr(bank[:, i * P:(i + 1) * P], xf[:, i, :], ident[:, :])
                    elif stage == "t_logits":
                        evacuated(["t_xfT"], part, b, into=stage)
                        for i in range(NT):
                            last = mm(bank[:, i * E:(i + 1) * E], xfT[:, i * P:(i + 1) * P], rw_sb[:, :],
                                      start=True, stop=True)
                    else:
                        pick, seen, w = ((picked_bf, seen_bf, 2 * E) if stage == "t_cum" else
                                         (mine_bf, filled_bf, E))
                        pe.wait_ge(s_picked if stage == "t_cum" else s_mine, b)
                        flat = "p a e -> p (a e)"
                        seen_all = seen[:, :, :].rearrange(flat) if stage == "t_cum" else seen[:, :]
                        for i in range(NT):
                            o = bank[:, i * w:(i + 1) * w]
                            of = [pick[:, m].rearrange(flat) if stage == "t_cum" else pick[:, m, :]
                                  for m in range(i + 1)]
                            mm(o, ones_bf[:, :], seen_all, start=True, stop=False)
                            for m in range(i):
                                mm(o, ones_bf[:, :], of[m], start=False, stop=False)
                            last = mm(o, upper_bf[:, :], of[i], start=False, stop=True)
                    last.then_inc(s_full[BANK[stage]], 1)

            parts(pe, body)

            pe.wait_ge(s_filled, NBATCH)
            pe.wait_ge(s_tfree, 12 * NBATCH)
            mm(tposed[0][:, 0:E], ones_bf[:, :], filled_bf[:, :], start=True, stop=True).then_inc(s_total, 1)
            pe.wait_ge(s_tab, 1)
            pe.wait_ge(s_moew, 16 * 3 * E)

            def x_transpose(t, k):
                pe.wait_ge(s_xb[k], 8 * t + (16 - 8 * k))
                wait(pe, s_xbT, t - 1)
                tr(scores[0][k][:, 0, 0:P], xb[k], ident[:, :]).then_inc(s_xbTp, 1)

            def go_up(t, k):
                e = pe.value_load(blk_tab[0:1, 0, bass.ds(t, 1)], min_val=0, max_val=E - 1)
                pe.wait_ge(s_xbT, t + 1)
                wait(pe, s_prod, t - 1)
                mm(scores[1][k][:, :, :].rearrange("p a b -> p (a b)"), xbT[k],
                   w12_sb[:, bass.ds(e, 1), :].rearrange("p a n -> p (a n)"), start=True, stop=True
                   ).then_inc(s_up, 1)

            def hid_transpose(t, k):
                pe.wait_ge(s_hid, t + 1)
                wait(pe, s_hT, t - 1)
                for m in range(2):
                    last = tr(tposed[k][:, m * P:(m + 1) * P], hid[k][:, m * P:(m + 1) * P], ident[:, :])
                last.then_inc(s_hTp, 1)

            def come_down(t, k):
                e = pe.value_load(blk_tab[0:1, 0, bass.ds(t, 1)], min_val=0, max_val=E - 1)
                pe.wait_ge(s_hT, t + 1)
                wait(pe, s_yb, t - 1)
                for m in range(2):
                    last = mm(shared[k][:, 0:D], hidT[k][:, m * P:(m + 1) * P],
                              w3_sb[:, bass.ds(e, 1), m, :].rearrange("p a d -> p (a d)"),
                              start=m == 0, stop=m == 1)
                last.then_inc(s_yp, 1)

            def step(t, k):
                n = t if isinstance(t, int) else None
                if n is None or n < NBLK:
                    x_transpose(t, k)
                if n is None or 1 <= n <= NBLK:
                    go_up(t - 1, 1 - k)
                if n is None or 2 <= n <= NBLK + 1:
                    hid_transpose(t - 2, k)
                if n is None or 3 <= n <= NBLK + 2:
                    come_down(t - 3, 1 - k)

            for t in range(4):
                step(t, t % 2)
            with pe.Fori(4, NBLK - 1, 2) as t:
                step(t, 0)
                step(t + 1, 1)
            for t in range(NBLK, NBLK + 3):
                step(t, t % 2)

        @block.scalar
        def _(act):
            act.wait_ge(s_const, 6 * 16)
            nc.scalar.activation(c_tmp[:, 0, :], c_sb[:, :], ACT.Exp, scale=-1.0).then_inc(s_setup_act, 1)
            act.wait_ge(s_w, 12 * 16)
            act.wait_ge(s_setup_dve, SETUP_ALL)

            def copied(ins, stage):
                ins.then_inc(s_free[BANK[stage]], 1)

            def exps(u, n):
                i, g = QUADS[u]
                act.wait_ge(s_negmax, 8 * n + (u + 1))
                t_before = sum(QUADS[m][0] + 1 for m in range(u - 1)) if u else -(QUADS[7][0] + 1)
                wait(act, s_tfull, 12 * n + t_before)
                for kv in range(HKV):
                    last = nc.scalar.activation(
                        probs[u % 2][:, kv, 0:(i + 1) * P], scores[u % 2][kv % 2][:, kv // 2, 0:(i + 1) * P],
                        ACT.Exp, bias=negmax[u % 2][:, kv % 2, kv // 2:kv // 2 + 1])
                last.then_inc(s_probs, 1)

            def body(part, b, k):
                n, nk = b + 1, 1 - k
                t_used = 0
                for kind, what in stages_of(part):
                    if kind == "scores":
                        if what in (8, 9) or part == "prologue":
                            exps(what % 8, n)
                        else:
                            exps(what, b)
                        continue
                    if kind == "transpose":
                        i, g = QUADS[what]
                        for at in range(i + 1):
                            act.wait_ge(s_tfull, 12 * b + (t_used + 1))
                            nc.scalar.copy(probsT[what % 2][:, 4 * at:4 * at + 4, :].rearrange("p m q -> p (m q)"),
                                           tposed[t_used % 2][:, :]).then_inc(s_tfree, 1)
                            t_used += 1
                        continue
                    if kind == "values":
                        continue
                    stage = what

                    def full():
                        act.wait_ge(s_full[BANK[stage]], uses_before(stage, part, b) + 1)

                    bank = shared[BANK["f_sa" if stage == "f_ea" else stage]] if (
                        stage == "f_ea" or stage not in NO_BANK) else None
                    if stage == "f_xnT":
                        full()
                        sl = span(n, 1)
                        copied(nc.scalar.activation(hT[:, :], bank[:, 0:T], ACT.Identity,
                                                    bias=modT[:, 0, sl], scale=modT[:, 1, sl]), stage)
                    elif stage == "f_qk":
                        full()
                        for j in range(2):
                            last = nc.scalar.activation(qkA[:, j, :], bank[:, j * T:(j + 1) * T], ACT.Identity,
                                                        bias=qk_bias[:, j:j + 1])
                        copied(last, stage)
                    elif stage == "f_ea":
                        act.wait_ge(s_biasA, n + 1)
                        for i in range(NT):
                            last = nc.scalar.activation(probsA[:, i * P:(2 * i + 1) * P],
                                                        bank[:, i * P:(2 * i + 1) * P], ACT.Exp,
                                                        bias=biasA[:, i:i + 1], scale=D ** -0.5,
                                                        accum_out=sumA[:, i:i + 1])
                        copied(last, "f_sa")
                    elif stage == "f_ta":
                        full()
                        copied(nc.scalar.copy(probsAT[:, :], bank[:, 0:3 * P]), stage)
                    elif stage == "f_ln2":
                        act.wait_ge(s_h2, n + 1)
                        for i in range(NT):
                            last = nc.scalar.activation(squares[:, i, :], h2[nk][:, i, :], ACT.Square,
                                                        accum_out=ms2[:, i:i + 1])
                        last.then_inc(s_ms2, 1)
                    elif stage == "f_xrT":
                        full()
                        copied(nc.scalar.activation(xrT[:, :], bank[:, 0:T], ACT.Identity, scale=g1_col[:, 0:1]),
                               stage)
                    elif stage[0:3] in ("f_k", "f_q"):
                        full()
                        i = int(stage[3])
                        if stage[2] == "k":
                            dst, m = kT[nk][:, :, i * P:(i + 1) * P], 2
                        else:
                            part4 = int(stage[4])
                            dst, m = qT[nk][:, 4 * part4:4 * part4 + 4, i * P:(i + 1) * P], 4
                        copied(nc.scalar.copy(dst, bank[:, 0:m * P].rearrange("p (m q) -> p m q", m=m)), stage)
                    elif stage.startswith("t_ot"):
                        full()
                        i, part4 = int(stage[4]), int(stage[5])
                        copied(nc.scalar.copy(attnT[:, 4 * part4:4 * part4 + 4, i * P:(i + 1) * P],
                                              bank[:, :].rearrange("p (m q) -> p m q", m=4)), stage)
                    elif stage == "t_sq":
                        act.wait_ge(s_free[BANK["t_wo"]], uses_before("t_wo", part, b) + 1)
                        for i in range(NT):
                            last = nc.scalar.activation(squares3[:, i, :], h[:, i, :], ACT.Square,
                                                        accum_out=ms3[:, i:i + 1])
                        last.then_inc(s_ms3, 1)
                    elif stage == "t_xfT":
                        full()
                        copied(nc.scalar.copy(xfT[:, :], bank[:, 0:T]), stage)
                    elif stage == "t_logits":
                        act.wait_ge(s_gap, b)
                        nc.scalar.activation(gap_exp[:, :], gap[:, :], ACT.Exp).then_inc(s_gexp, 1)

            parts(act, body)

            def step(t, k):
                n = t if isinstance(t, int) else None
                if n is None or n < NBLK:
                    act.wait_ge(s_xbTp, t + 1)
                    wait(act, s_up, t - 1)
                    nc.scalar.copy(xbT[k], scores[0][k][:, 0, 0:P]).then_inc(s_xbT, 1)
                if n is None or 1 <= n <= NBLK:
                    act.wait_ge(s_up, t)
                    wait(act, s_prod, t - 2)
                    nc.scalar.copy(up[1 - k], scores[1][1 - k][:, 0, :]).then_inc(s_upc, 1)
                    act.wait_ge(s_prod, t)
                    wait(act, s_hTp, t - 2)
                    nc.scalar.activation(hid[1 - k], prod[1 - k], ACT.Gelu).then_inc(s_hid, 1)

            act.wait_ge(s_tab, 1)
            for t in range(4):
                step(t, t % 2)
            with act.Fori(4, NBLK - 1, 2) as t:
                step(t, 0)
                step(t + 1, 1)
            step(NBLK, 0)

        @block.gpsimd
        def _(pool):
            half = small[:, C_HALF:C_HALF + NT]
            nc.gpsimd.memset(zeros[:, :], 0.0).then_inc(s_zeros, 1)
            pool.wait_ge(s_const, 6 * 16)
            pool.wait_ge(s_zero, ZEROED)

            def rsqrt(dst, tmp, src, scale, eps, sem_in, value, sem_mid, sem_out):
                wait_alone(pool, sem_in, value, CONSTS)
                nc.gpsimd.tensor_scalar(tmp, src, scale, eps, ALU.mult, ALU.add).then_inc(sem_mid, 1)
                pool.wait_ge(sem_mid, value)
                nc.gpsimd.tensor_tensor(dst, tmp, half, ALU.pow).then_inc(sem_out, 1)

            def body(part, b, k):
                n, nk = b + 1, 1 - k
                for kind, what in stages_of(part):
                    if kind != "stage":
                        continue
                    stage = what
                    if stage == "f_stats":
                        rsqrt(rstd[:, :], var_eps[:, :], mv[:, :, 1], 1.0, 1e-5, s_var, n + 1, s_vareps, s_rstd)
                    elif stage == "f_pva":
                        rsqrt(rstd2[:, :], var2_eps[:, :], mv2[:, :, 1], 1.0, 1e-5, s_var2, n + 1, s_var2eps,
                              s_rstd2)
                    elif stage == "f_ln2":
                        rsqrt(rms2[:, :], ms2_eps[:, :], ms2[:, :], 1.0 / D, 1e-6, s_ms2, n + 1, s_ms2eps,
                              s_rms2)
                    elif stage.startswith("f_p"):
                        i, j = int(stage[3]), "kab".index(stage[4])
                        m = 3 * i + j
                        heads = (HQ, HKV) if j == 0 else (8 * (j - 1), 8)
                        pool.wait_ge(s_free[BANK[stage]], uses_before(stage, part, b) + 1)
                        src = slice(0, heads[1] * K)
                        nc.gpsimd.tensor_tensor(
                            qtok[:, i, heads[0]:heads[0] + heads[1], :].rearrange("p h d -> p (h d)"),
                            rope_cos[m % 2][:, src], rope_sin[m % 2][:, src], ALU.add).then_inc(s_roped, 1)
                    elif stage == "t_sq":
                        rsqrt(rms3[:, :], ms3_eps[:, :], ms3[:, :], 1.0 / D, 1e-6, s_ms3, b, s_ms3eps, s_rms3)
                    elif stage == "t_base":
                        wait_alone(pool, s_sidx, b, CONSTS)
                        for i in range(NT):
                            nc.gpsimd.indirect_dma_start(
                                out=xs_dram, out_offset=bass.IndirectOffsetOnAxis(ap=scatter_idx[:, i:i + 1], axis=0),
                                in_=xf[:, i, :], in_offset=None).then_inc(s_scat, 16)

            parts(pool, body)

            for k in range(2):
                pool.wait_ge(s_ys[k], 16 * NBLK // 2)

            def gather(b, k):
                for i in range(NT):
                    nc.gpsimd.indirect_dma_start(
                        out=yg[k][:, i, :], out_offset=None, in_=ys_dram[0:DUMP, :],
                        in_offset=bass.IndirectOffsetOnAxis(ap=gather_pair[k][:, i:i + 1], axis=0)
                    ).then_inc(s_yg[k], 16)

            for b in range(2):
                pool.wait_ge(s_gidx, b + 1)
                gather(b, b)
            with pool.Fori(2, NBATCH - 1, 2) as b:
                for k in range(2):
                    wait_alone(pool, s_gidx, b + (k + 1), CONSTS)
                    gather(b + k, k)

        @block.vector
        def _(dve):
            v = nc.vector
            tt, ts, stt = v.tensor_tensor, v.tensor_scalar, v.scalar_tensor_tensor
            count = {}

            def link(ins, sem_, base=0, alone=False):
                ins.then_inc(sem_, 1)
                count[id(sem_)] = count.get(id(sem_), 0) + 1
                if alone:
                    wait_alone(dve, sem_, base + count[id(sem_)], CONSTS)
                else:
                    dve.wait_ge(sem_, base + count[id(sem_)])

            v.memset(ones_bf[:, :], 1.0)
            v.memset(seen_bf[:, :, :], 0.0)
            v.memset(filled_bf[:, :], 0.0)
            for k in range(2):
                v.memset(v1[k][:, :, :, K:K + 1], 1.0)
            dve.wait_ge(s_const, 6 * 16)
            v.tensor_copy(mask_bf[:, :], stage_f32[:, 0, :])
            v.tensor_copy(upper_bf[:, :], stage_f32[:, 1, :])
            v.tensor_copy(ident_bf[:, :], ident[:, :])
            dve.wait_ge(s_setup_act, 1)
            link(ts(c_tmp[:, 1, :], c_tmp[:, 0, :], 1.0, None, ALU.add), s_setup_dve)
            link(v.reciprocal(c_tmp[:, 0, :], c_tmp[:, 1, :]), s_setup_dve)
            link(tt(c_tmp[:, 1, :], c_tmp[:, 0, :], c_sb[:, :], ALU.mult), s_setup_dve)
            dve.wait_ge(s_setup_pe, 1)
            link(v.tensor_copy(scT[:, :], shared[0][:, 0:NBATCH]), s_setup_dve)
            dve.wait_ge(s_setup_pe, 2)
            mod_ps = shared[1][0:NBATCH, :].rearrange("b (j d) -> b j d", j=4)
            v.tensor_copy(mod_rows[:, SB, :], mod_ps[:, 1, :])
            ts(mod_rows[:, CB, :], mod_ps[:, 2, :], 1.0, None, ALU.add)
            gates = mod_ps[:, 0:4:3, :]
            link(ts(mod_sign[:, :, :], gates, 0.0, 2.0, ALU.is_ge, ALU.mult), s_setup_dve)
            link(ts(mod_sign[:, :, :], mod_sign[:, :, :], 1.0, None, ALU.subtract), s_setup_dve)
            link(tt(mod_mag[:, :, :], gates, mod_sign[:, :, :], ALU.mult), s_setup_dve)
            link(stt(mod_rows[:, 0:4:3, :], mod_mag[:, :, :], 0.25, mod_sign[:, :, :], ALU.max, ALU.mult),
                 s_setup_dve)
            dve.wait_ge(s_setup_pe, 3)
            v.tensor_copy(modT[:, 0, :], shared[0][:, 0:NBATCH])
            link(ts(modT[:, 1, :], shared[0][:, NBATCH:2 * NBATCH], 1.0, None, ALU.add), s_setup_dve)
            assert count[id(s_setup_dve)] == SETUP_ALL
            dve.wait_ge(s_w, 12 * 16)

            def copied(ins, stage):
                ins.then_inc(s_free[BANK[stage]], 1)

            def norm(dst, src, mv_, rstd_):
                for i in range(NT):
                    last = ts(dst[:, i, :], src(i), mv_[:, i, 0:1], rstd_[:, i:i + 1], ALU.subtract, ALU.mult)
                return last

            def body(part, b, k):
                n, nk = b + 1, 1 - k
                count.clear()
                seen_stages = set()

                def full(stage):
                    dve.wait_ge(s_full[BANK[stage]], uses_before(stage, part, b) + 1)

                def flink(ins, alone=False):
                    link(ins, s_dfront, FRONT_LINKS * n, alone)

                def tlink(ins):
                    link(ins, s_dtail, TAIL_LINKS * (b - 1))

                def mod(j, m):
                    return mod_all[:, span(m, 1), j, :]

                for kind, what in stages_of(part):
                    if kind == "transpose":
                        continue
                    if kind == "scores":
                        m = n if (what >= 8 or part == "prologue") else b
                        u = what % 8
                        i, g = QUADS[u]
                        dve.wait_ge(s_scores, 8 * m + (u + 1))
                        for half in range(2):
                            last = v.tensor_reduce(negmax[u % 2][:, half, :],
                                                   scores[u % 2][half][:, :, 0:(i + 1) * P],
                                                   AX_X, ALU.max, negate=True)
                        last.then_inc(s_negmax, 1)
                        continue
                    if kind == "values":
                        i, g = QUADS[what]
                        full(f"pv{what}")
                        o = shared[BANK[f"pv{what}"]][:, 0:HKV * (K + 1)].rearrange("p (h d) -> p h d", h=HKV)
                        link(v.reciprocal(rden[:, :], o[:, :, K]), s_dattn, ATTN_LINKS * b)
                        last = tt(attn[:, i, 4 * g * K:(4 * g + 4) * K].rearrange("p (h d) -> p h d", h=HKV),
                                  o[:, :, 0:K], rden[:, :].unsqueeze(2).to_broadcast([P, HKV, K]), ALU.mult)
                        copied(last, f"pv{what}")
                        continue
                    stage = what
                    bank = shared[BANK[stage]] if stage not in NO_BANK else None
                    if stage == "f_stats":
                        wait_alone(dve, s_x[nk], 8 * n + (16 - 8 * nk), CONSTS)
                        for i in range(NT):
                            last = v.bn_stats(stats[:, i, :], x_in[nk][:, i, :])
                        link(last, s_dstats, STATS_LINKS * n, alone=True)
                        for i in range(NT):
                            last = v.bn_aggr(mv[:, i, :], stats[:, i, :])
                        last.then_inc(s_var, 1)
                        dve.wait_ge(s_rstd, n + 1)
                        norm(xn, lambda i: x_in[nk][:, i, :], mv, rstd).then_inc(s_xn, 1)
                    elif stage == "f_va":
                        full(stage)
                        copied(tt(vA[:, :, :], bank[:, 0:NT * D].rearrange("p (i d) -> p i d", i=NT),
                                  bv_bc[:, :].unsqueeze(1).to_broadcast([P, NT, D]), ALU.add), stage)
                    elif stage == "f_sa":
                        full(stage)
                        for i in range(NT):
                            last = v.tensor_reduce(biasA[:, i:i + 1], bank[:, i * P:(2 * i + 1) * P], AX_X,
                                                   ALU.max, negate=True)
                        flink(last)
                        ts(biasA[:, :], biasA[:, :], D ** -0.5, None, ALU.mult).then_inc(s_biasA, 1)
                    elif stage == "f_pva":
                        dve.wait_ge(s_free[BANK["f_sa"]], uses_before("f_sa", part, b) + 1)
                        flink(v.reciprocal(rsumA[:, :], sumA[:, :]))
                        full(stage)
                        if part == "prologue":
                            dve.wait_ge(s_modin, 16 * 4)
                        for i in range(NT):
                            last = stt(attA[:, i:i + 1, :], bank[:, i * P:(i + 1) * P].unsqueeze(1),
                                       rsumA[:, i:i + 1], mod(GA, n), ALU.mult, ALU.mult)
                        last.then_inc(s_free[BANK[stage]], 1)
                        dve.wait_ge(s_free[BANK[stage]], uses_before(stage, part, b) + 1)
                        ins = tt(base_all[:, span(2 * n, NT), :], attA[:, :, :], x_in[nk][:, :, :], ALU.add)
                        ins.then_inc(s_x2, 1)
                        wait_alone(dve, s_x2, n + 1, CONSTS)
                        for i in range(NT):
                            last = v.bn_stats(stats2[:, i, :], base_all[:, span(2 * n + i, 1), :])
                        flink(last, alone=True)
                        for i in range(NT):
                            last = v.bn_aggr(mv2[:, i, :], stats2[:, i, :])
                        last.then_inc(s_var2, 1)
                    elif stage == "f_ln2":
                        dve.wait_ge(s_rstd2, n + 1)
                        flink(norm(xn2, lambda i: base_all[:, span(2 * n + i, 1), :]
                                   .rearrange("p a d -> p (a d)"), mv2, rstd2))
                        flink(tt(xn2[:, :, :], xn2[:, :, :], mod(CB, n).to_broadcast([P, NT, D]), ALU.mult))
                        tt(h2[nk][:, :, :], xn2[:, :, :], mod(SB, n).to_broadcast([P, NT, D]), ALU.add
                           ).then_inc(s_h2, 1)
                    elif stage == "f_rms":
                        dve.wait_ge(s_rms2, n + 1)
                        dve.wait_ge(s_h2, n + 1)
                        for i in range(NT):
                            last = ts(xr[:, i, :], h2[nk][:, i, :], rms2[:, i:i + 1], None, ALU.mult)
                        last.then_inc(s_xr, 1)
                    elif stage.startswith("f_p"):
                        i, j = int(stage[3]), "kab".index(stage[4])
                        m = 3 * i + j
                        heads = HKV if j == 0 else 8
                        tab = 2 if j == 0 else 0
                        full(stage)
                        wait(dve, s_roped, 6 * n + (m - 1))
                        if j == 0:
                            v.tensor_copy(v1[nk][:, i, :, 0:K], bank[:, HKV * K:].rearrange(
                                "p (h d) -> p h d", h=HKV)).then_inc(s_v1, 1)
                        q = bank[:, 0:heads * K].rearrange("p (h d) -> p h d", h=heads)
                        cos, sin = (r[m % 2][:, 0:heads * K].rearrange("p (h d) -> p h d", h=heads)
                                    for r in (rope_cos, rope_sin))

                        def table(w, lo, hi):
                            return rope[:, tab + w, i, lo:hi].unsqueeze(1).to_broadcast([P, heads, hi - lo])

                        tt(cos, q, table(0, 0, K), ALU.mult)
                        tt(sin[:, :, 0:K // 2], q[:, :, K // 2:K], table(1, 0, K // 2), ALU.mult)
                        last = tt(sin[:, :, K // 2:K], q[:, :, 0:K // 2], table(1, K // 2, K), ALU.mult)
                        copied(last, stage)
                    elif stage == "t_wo":
                        full(stage)
                        last = tt(h[:, :, :], bank[:, 0:NT * D].rearrange("p (i d) -> p i d", i=NT),
                                  h2[1 - k][:, :, :], ALU.add)
                        copied(last, stage)
                    elif stage == "t_xf":
                        dve.wait_ge(s_rms3, b)
                        dve.wait_ge(s_free[BANK["t_wo"]], uses_before("t_wo", part, b) + 1)
                        wait(dve, s_scat, 16 * NT * (b - 1))
                        for i in range(NT):
                            last = stt(xf[:, i, :], h[:, i, :], rms3[:, i:i + 1], g2_bc[:, :], ALU.mult, ALU.mult)
                        last.then_inc(s_xf, 1)
                    elif stage == "t_logits":
                        full(stage)
                        last = tt(logits[:, :, :], bank[:, 0:NT * E].rearrange("p (i e) -> p i e", i=NT),
                                  rb_bc[:, :].unsqueeze(1).to_broadcast([P, NT, E]), ALU.add)
                        last.then_inc(s_free[BANK[stage]], 1)
                        wait_alone(dve, s_free[BANK[stage]], uses_before(stage, part, b) + 1, CONSTS)
                        for i in range(NT):
                            last = v.max(top8[:, i, :], logits[:, i, :])
                        tlink(last)
                        tt(gap[:, :], top8[:, :, 1], top8[:, :, 0], ALU.subtract).then_inc(s_gap, 1)
                        for i in range(NT):
                            last = v.max_index(idx8[:, i, :], top8[:, i, :], logits[:, i, :])
                        tlink(last)
                        tlink(v.tensor_copy(idxf[:, :, :], idx8[:, :, 0:2]))
                        ik = "p i k e -> p (i k) e"
                        tlink(tt(picked[:, :, :, :].rearrange(ik), iota8.unsqueeze(1).to_broadcast([P, NT * 2, E]),
                                 idxf[:, :, :].rearrange("p i k -> p (i k)").unsqueeze(2)
                                 .to_broadcast([P, NT * 2, E]), ALU.is_equal))
                        v.tensor_copy(picked_bf[:, :, 0, :], picked[:, :, 0, :])
                        tt(picked_bf[:, :, 1, :], picked[:, :, 0, :], picked[:, :, 1, :], ALU.add
                           ).then_inc(s_picked, 1)
                    elif stage == "t_cum":
                        full(stage)
                        last = stt(kept[:, :, :, :].rearrange("p i k e -> p (i k e)"), bank[:, 0:NT * 2 * E],
                                   float(CAP), picked[:, :, :, :].rearrange("p i k e -> p (i k e)"),
                                   ALU.is_lt, ALU.mult)
                        last.then_inc(s_free[BANK[stage]], 1)
                        dve.wait_ge(s_free[BANK[stage]], uses_before(stage, part, b) + 1)
                        tlink(tt(seen_bf[:, :, :], seen_bf[:, :, :], picked_bf[:, 0], ALU.add))
                        tlink(tt(seen_bf[:, :, :], seen_bf[:, :, :], picked_bf[:, 1], ALU.add))
                        ik = "p i k e -> p (i k) e"
                        v.tensor_reduce(kept_any[:, :, :].rearrange("p i k -> p (i k)"),
                                        kept[:, :, :, :].rearrange(ik), AX_X, ALU.add)
                        tlink(tt(kept_id[:, :, :, :].rearrange(ik), kept[:, :, :, :].rearrange(ik),
                                 iota8.unsqueeze(1).to_broadcast([P, NT * 2, E]), ALU.mult))
                        tlink(v.tensor_reduce(kept_expert[:, :, :].rearrange("p i k -> p (i k)"),
                                              kept_id[:, :, :, :].rearrange(ik), AX_X, ALU.add))
                        tt(has[:, :], kept_any[:, :, 0], kept_any[:, :, 1], ALU.max)
                        tlink(tt(expert[:, :], kept_expert[:, :, 0], kept_expert[:, :, 1], ALU.max))
                        tlink(tt(mine[:, :, :], iota8.unsqueeze(1).to_broadcast([P, NT, E]),
                                 expert[:, :].unsqueeze(2).to_broadcast([P, NT, E]), ALU.is_equal))
                        tt(mine_bf[:, :, :], mine[:, :, :], has[:, :].unsqueeze(2).to_broadcast([P, NT, E]),
                           ALU.mult).then_inc(s_mine, 1)
                        dve.wait_ge(s_gexp, b)
                        tlink(ts(gap_den[:, :], gap_exp[:, :], 1.0, None, ALU.add))
                        tlink(v.reciprocal(score[:, :, 0], gap_den[:, :]))
                        tlink(tt(score[:, :, 1], score[:, :, 0], gap_exp[:, :], ALU.mult))
                        tlink(tt(kept_score[:, :, :], kept_any[:, :, :], score[:, :, :], ALU.mult))
                        v.tensor_reduce(score_all[:, span(2 * (b - 1), NT)], kept_score[:, :, :], AX_X, ALU.add)
                        tlink(tt(score[:, :, :], score[:, :, :], kept_score[:, :, :], ALU.subtract))
                        tlink(v.tensor_reduce(drop_score[:, :], score[:, :, :], AX_X, ALU.add))
                    elif stage == "t_rank":
                        full(stage)
                        last = tt(rank_of[:, :, :], bank[:, 0:NT * E].rearrange("p (i e) -> p i e", i=NT),
                                  mine_bf[:, :, :], ALU.mult)
                        last.then_inc(s_free[BANK[stage]], 1)
                        dve.wait_ge(s_free[BANK[stage]], uses_before(stage, part, b) + 1)
                        tlink(tt(filled_bf[:, :], filled_bf[:, :], mine_bf[:, 0, :], ALU.add))
                        tt(filled_bf[:, :], filled_bf[:, :], mine_bf[:, 1, :], ALU.add).then_inc(s_filled, 1)
                        tlink(v.tensor_reduce(rank[:, :], rank_of[:, :, :], AX_X, ALU.add))
                        tlink(stt(row[:, :], expert[:, :], float(ROWS), rank[:, :], ALU.mult, ALU.add))
                        ts(dump_row[:, :], has[:, :], -1.0, 1.0, ALU.mult, ALU.add)
                        tlink(stt(row[:, :], row[:, :], -1.0, has[:, :], ALU.add, ALU.mult))
                        tlink(tt(dump_row[:, :], dump_row[:, :], small[:, span(2 * b + (C_DUMP - 2), NT)], ALU.mult))
                        v.tensor_copy(gather_all[:, span(2 * b - 2, NT)], row[:, :])
                        tt(scatter_idx[:, :], row[:, :], dump_row[:, :], ALU.add).then_inc(s_sidx, 1)
                    elif stage == "t_base":
                        for i in range(NT):
                            last = stt(base_tmp[:, i, :], xf[:, i, :], drop_score[:, i:i + 1], h[:, i, :],
                                       ALU.mult, ALU.add)
                        tlink(last)
                        tlink(tt(base_tmp[:, :, :], base_tmp[:, :, :],
                                 mod(GB, b - 1).to_broadcast([P, NT, D]), ALU.mult))
                        rows = base_all[:, span(2 * b - 2, NT), :]
                        tlink(tt(rows, rows, base_tmp[:, :, :], ALU.add))
                for s_, size in ((s_dfront, FRONT_LINKS), (s_dattn, ATTN_LINKS), (s_dtail, TAIL_LINKS),
                                 (s_dstats, STATS_LINKS)):
                    assert count.get(id(s_), size) == size, (part, count[id(s_)], size)

            parts(dve, body)

            def elink(ins):
                link(ins, s_dend)

            count.clear()
            dve.wait_ge(s_total, 1)
            thr = small[:, C_THR:C_THR + E * E].rearrange("p (e k) -> p e k", e=E)
            lower = small[:, C_LOWER:C_LOWER + E * E].rearrange("p (e f) -> p e f", e=E)
            number = small[:, C_BLK:C_BLK + NBLK]
            elink(tt(blk_need[:, :, :], tposed[0][:, 0:E].unsqueeze(2).to_broadcast([P, E, E]), thr, ALU.is_gt))
            elink(v.tensor_reduce(blk_cnt[:, :], blk_need[:, :, :], AX_X, ALU.add))
            elink(tt(blk_need[:, :, :], lower, blk_cnt[:, :].unsqueeze(1).to_broadcast([P, E, E]), ALU.mult))
            elink(v.tensor_reduce(blk_cum[:, :], blk_need[:, :, :], AX_X, ALU.add))
            elink(tt(blk_past[:, :, :], blk_cum[:, :].unsqueeze(1).to_broadcast([P, NBLK, E]),
                     number.unsqueeze(2).to_broadcast([P, NBLK, E]), ALU.is_le))
            v.tensor_reduce(blk_f[:, 0, :], blk_past[:, :, :], AX_X, ALU.add)
            elink(tt(blk_pastn[:, :, :], blk_past[:, :, :], blk_cnt[:, :].unsqueeze(1).to_broadcast([P, NBLK, E]),
                     ALU.mult))
            elink(v.tensor_reduce(blk_f[:, 1, :], blk_pastn[:, :, :], AX_X, ALU.add))
            ts(blk_f[:, 2, :], blk_f[:, 0, :], float(E), None, ALU.is_lt)
            elink(tt(blk_f[:, 3, :], number, blk_f[:, 1, :], ALU.subtract))
            elink(stt(blk_f[:, 4, :], blk_f[:, 0, :], float(ROWS // P), blk_f[:, 3, :], ALU.mult, ALU.add))
            elink(stt(blk_f[:, 5, :], blk_f[:, 4, :], float(P), blk_f[:, 2, :], ALU.mult, ALU.mult))
            elink(ts(blk_f[:, 6, :], number, float(P), float(DUMP), ALU.mult, ALU.add))
            elink(ts(blk_f[:, 7, :], blk_f[:, 2, :], -1.0, 1.0, ALU.mult, ALU.add))
            elink(tt(blk_f[:, 7, :], blk_f[:, 7, :], blk_f[:, 6, :], ALU.mult))
            tt(blk_tab[:, 0, :], blk_f[:, 0, :], blk_f[:, 2, :], ALU.mult)
            v.tensor_copy(blk_tab[:, 1, :], blk_f[:, 5, :])
            tt(blk_tab[:, 2, :], blk_f[:, 5, :], blk_f[:, 7, :], ALU.add).then_inc(s_tab, 1)

            def step(t, k):
                m = t if isinstance(t, int) else None
                if m is None or 3 <= m <= NBLK + 2:
                    dve.wait_ge(s_yp, t - 2)
                    wait(dve, s_ys[1 - k], 8 * (t - 3) - 8 * (1 - k))
                    v.tensor_copy(yb[1 - k], shared[1 - k][:, 0:D]).then_inc(s_yb, 1)
                if m is None or 2 <= m <= NBLK + 1:
                    dve.wait_ge(s_hTp, t - 1)
                    wait(dve, s_yp, t - 3)
                    v.tensor_copy(hidT[k], tposed[k][:, 0:HID]).then_inc(s_hT, 1)
                if m is None or 1 <= m <= NBLK:
                    dve.wait_ge(s_upc, t)
                    wait(dve, s_hid, t - 2)
                    tt(prod[1 - k], scores[1][1 - k][:, 1, :], up[1 - k], ALU.mult).then_inc(s_prod, 1)

            for t in range(1, 4):
                step(t, t % 2)
            with dve.Fori(4, NBLK - 1, 2) as t:
                step(t, 0)
                step(t + 1, 1)
            for t in range(NBLK, NBLK + 3):
                step(t, t % 2)

            def gather_rows(b, k):
                v.tensor_copy(gather_pair[k][:, :], gather_all[:, span(2 * b, NT)]).then_inc(s_gidx, 1)

            def finish(b, k, more):
                dve.wait_ge(s_yg[k], 16 * b + (32 - 16 * k))
                wait(dve, s_out[k], 8 * b - 8 * k)
                for i in range(NT):
                    last = stt(yo[k][:, i:i + 1, :], yg[k][:, i:i + 1, :], score_all[:, span(2 * b + i, 1)],
                               mod_all[:, span(b, 1), GB, :], ALU.mult, ALU.mult)
                last.then_inc(s_scaled, 1)
                dve.wait_ge(s_scaled, b + 1)
                if more:
                    gather_rows(b + 2, k)
                tt(yo[k], yo[k], base_all[:, span(2 * b, NT), :], ALU.add).then_inc(s_yo, 1)

            for k in range(2):
                gather_rows(k, k)
            with dve.Fori(0, NBATCH - 3, 2) as b:
                finish(b, 0, True)
                finish(b + 1, 1, True)
            for k in range(2):
                finish(NBATCH - 2 + k, k, False)


_INS = ["L0_attn_x", "L0_attn_W", "L0_attn_b", "L0_ffn_g1", "L0_ffn_g2", "L0_ffn_wq", "L0_ffn_wk", "L0_ffn_wv",
        "L0_ffn_wo", "L0_ffn_router_w", "L0_ffn_router_b", "L0_ffn_w1", "L0_ffn_w2", "L0_ffn_w3", "L0_c",
        "L0_wmod"]


def shape_constants():
    f32 = np.float32
    rows = np.arange(P)
    ident = np.eye(P, dtype=f32)
    mask = np.where(rows[None, :] > rows[:, None], f32(MASKED), f32(0)).astype(f32)
    upper = (rows[:, None] <= rows[None, :]).astype(f32)
    thetas = 10000.0 ** (-np.arange(0, K, 2, dtype=f32) / K)
    ticks = np.tile(np.outer(np.arange(T, dtype=f32), thetas), (1, 2))
    cos = np.cos(ticks).astype(f32)
    sin = np.sin(ticks).astype(f32)
    sin[:, :K // 2] *= -1
    scale = f32(K ** -0.5)
    tables = np.stack([cos * scale, sin * scale, cos, sin])
    rope = np.ascontiguousarray(tables.reshape(4, NT, P, K).transpose(2, 0, 1, 3))
    small = np.zeros((P, C_END), f32)
    small[:, C_IOTA8:C_IOTA8 + E] = np.arange(E)
    small[:, C_DUMP:C_DUMP + NBATCH * NT] = DUMP + P * np.arange(NBATCH * NT)[None, :] + rows[:, None]
    small[:, C_THR:C_THR + E * E] = np.tile(P * np.arange(E), E)
    small[:, C_LOWER:C_LOWER + E * E] = np.tril(np.ones((E, E))).ravel()
    small[:, C_BLK:C_BLK + NBLK] = np.arange(NBLK)
    small[:, C_HALF:C_HALF + 2] = -0.5
    return {"k_ident": ident, "k_mask": mask, "k_upper": upper, "k_rope": rope, "k_small": small}


def kernel(**inputs):
    import numpy as _np
    import concourse.bacc as _bacc
    from concourse import mybir as _mybir
    from concourse.bass_utils import run_bass_kernel_spmd as _run

    nc = _bacc.Bacc("TRN2", target_bir_lowering=False, num_devices=1)
    arrays, args = {}, []
    for name, a in [(n, inputs[n]) for n in _INS] + list(shape_constants().items()):
        a = _np.ascontiguousarray(a)
        arrays[f"in_{name}"] = a
        args.append(nc.dram_tensor(f"in_{name}", a.shape, _mybir.dt.from_np(a.dtype), kind="ExternalInput").ap())
    args.append(nc.dram_tensor("out_dram", (NBATCH, T, D), F32, kind="ExternalOutput").ap())
    adaln_layer(nc, *args)
    r = _run(nc, [arrays], core_ids=[0])
    return r.results[0]["out_dram"]
```

```python
from contextlib import ExitStack

import numpy as np

import concourse.bass as bass
from concourse import mybir

ALU = mybir.AluOpType
ACT = mybir.ActivationFunctionType
F32 = mybir.dt.float32
BF16 = mybir.dt.bfloat16
U32 = mybir.dt.uint32
I32 = mybir.dt.int32
AX_X = mybir.AxisListType.X

P = 128
NBATCH, T, D = 16, 256, 128
NT = T // P
HQ, HKV, K = 16, 4, 64
QKV = (HQ + 2 * HKV) * K
NCH = HQ * K // P
E, HID = 8, 256
NTOK = NBATCH * T
CAP = NTOK // 8
ROWS = 2 * CAP
DUMP = E * ROWS
NBLK = 40
MASKED = -1e30

C_IOTA8 = 0
C_DUMP = 8
C_THR = C_DUMP + NBATCH * NT
C_LOWER = C_THR + 64
C_BLK = C_LOWER + 64
C_HALF = C_BLK + NBLK
C_TOKEN = C_HALF + 2
C_PAST = C_TOKEN + NBATCH * NT
C_END = C_PAST + NBLK

ROW = D + 4
SPARE = DUMP + NTOK
FILL = 8
ZEROED = 16 * 3
LOADED_A, LOADED_F, LOADED_T = 16 * 3, 16 * 5, 16 * 4
XBUFS = 4
YBUFS = 4
OUTS = 2
POOL_OUTS = (2, 5)
SETUP_SILU, SETUP_SCT, SETUP_MOD, SETUP_ALL = 3, 4, 8, 9
STATS_LINKS, FRONT_LINKS, TAIL_LINKS = 1, 4, 24

QUADS = [(i, g) for g in range(4) for i in range(NT)]

SLOTS = [
    ("transpose0", "normalize1", "t_wo0", "a_stats", "f_xrT", "scores2", "a_rstd", "max2", "exps2", "values0",
     "f_p0k", "f_r0k", "normalize2", "a_xn"),
    ("transpose1", "f_r0a", "f_p0b", "f_p0a", "scores3", "max3", "a_xnT", "exps3", "t_wo1", "t_rms", "f_r0b",
     "values1", "t_sq", "t_xf", "normalize3"),
    ("transpose2", "f_r1k", "f_q00T", "f_k0T", "scores4", "values2", "a_qk", "f_p1k", "t_xfT"),
    ("exps4", "scores5", "max4", "transpose3", "a_va", "max5", "t_logits", "f_p1a", "normalize4", "f_r1a",
     "values3", "exps5", "f_q01T", "a_sa", "normalize5"),
    ("transpose4", "a_ea", "scores6", "f_r1b", "max6", "f_p1b", "values4", "t_top", "exps6", "max7",
     "normalize6"),
    ("scores7", "a_ta", "f_k1T", "t_gexp", "t_cum", "transpose5", "f_q10T", "t_keep", "a_pva", "normalize7"),
    ("a_rstd2", "exps7", "values5", "transpose6", "a_x2", "f_q11T", "scores8", "max8", "values6", "a_ln2",
     "exps8", "a_rms", "a_sq", "t_rank", "t_score", "normalize8"),
    ("scores9", "t_row", "a_xr", "transpose7", "exps9", "values7", "t_send", "max9", "t_base"),
]
NO_BANK = ("a_stats", "a_rstd", "a_xn", "a_ea", "a_x2", "a_rstd2", "a_ln2", "a_sq", "a_rms", "a_xr", "f_r0k", "f_r0a",
           "f_r0b", "f_r1k", "f_r1a", "f_r1b", "t_sq", "t_rms", "t_xf", "t_top", "t_gexp", "t_keep", "t_score",
           "t_row", "t_base", "t_send")
LAG = {"a": 2, "f": 1, "q": 0, "t": -1}
BODIES = range(-LAG["a"], NBATCH - LAG["t"])
MIDDLE = 1


def runs(kind, b):
    return not isinstance(b, int) or 0 <= b + LAG[kind] < NBATCH


def stages_of(b):
    for slot in SLOTS:
        for s in slot:
            kind, quad = s[:-1], s[-1]
            if kind in ("scores", "max", "exps", "normalize", "transpose", "values"):
                if runs("q" if int(quad) < 8 else "f", b):
                    yield kind, int(quad)
            elif runs(s[0], b):
                yield "stage", s


def transposes_to(u):
    return sum(QUADS[m][0] + 1 for m in range(u))


def shared_order(b):
    return [f"pv{s}" if kind == "values" else s for kind, s in stages_of(b)
            if kind == "values" or kind == "stage" and s not in NO_BANK]


BANK = {s: n % 2 for n, s in enumerate(shared_order(MIDDLE))}


def uses_before(stage, b):
    bank = BANK[stage]
    at = b if isinstance(b, int) else MIDDLE
    n = [sum(BANK[s] == bank for s in shared_order(m)) for m in BODIES if m < at]
    order = shared_order(at)
    here = sum(n) + sum(BANK[s] == bank for s in order[:order.index(stage)])
    if isinstance(b, int):
        return here
    per_body = sum(BANK[s] == bank for s in order)
    return b * per_body + (here - MIDDLE * per_body)


def span(start, size):
    return slice(start, start + size) if isinstance(start, int) else bass.ds(start, size)


def wait(eng, sem, value):
    if isinstance(value, int) and value <= 0:
        return
    eng.wait_ge(sem, value)


def wait_alone(eng, sem, value, held):
    if not isinstance(value, int):
        value = eng.snap(eng.to_reg(value))
        eng.wait_ge(*held)
    eng.wait_ge(sem, value)


def bodies(eng, body):
    for b in range(-2, 2):
        body(b, b % 2)
    with eng.Fori(2, NBATCH - 3, 2) as b:
        body(b, 0)
        body(b + 1, 1)
    for b in range(NBATCH - 2, NBATCH + 1):
        body(b, b % 2)


def steps(eng, step):
    for t in range(12):
        step(t, t % 4)
    with eng.Fori(12, NBLK - 3, 4) as t:
        for k in range(4):
            step(t + k, k)
    for t in range(NBLK, NBLK + 7):
        step(t, t % 4)


def has_block(t, lag):
    return not isinstance(t, int) or 0 <= t - lag < NBLK


def adaln_layer(nc, x, W, bias, g1, g2, wq, wk, wv, wo, router_w, router_b, w1, w2, w3, c, wmod,
                k_ident, k_mask, k_upper, k_rope, k_small, out):
    ctx = ExitStack()
    with ctx:
        def sb(name, shape, dt=F32):
            return ctx.enter_context(nc.sbuf_tensor(name, shape, dt))

        def pb(name, shape):
            return ctx.enter_context(nc.psum_tensor(name, shape, F32))

        def sem(name):
            return ctx.enter_context(nc.semaphore(name))

        xs_dram = nc.dram_tensor("expert_rows", (SPARE + P, ROW), F32, kind="Internal").ap()
        ys_dram = nc.dram_tensor("results_by_token", (NTOK + NBLK * P, D), F32, kind="Internal").ap()
        mod_dram = nc.dram_tensor("modulation_rows", (NBATCH, 4 * D), F32, kind="Internal").ap()

        ident = sb("ident", [P, P])
        stage_f32 = sb("stage_f32", [P, 2, P])
        mask_bf = sb("mask_bf", [P, P], BF16)
        ident_bf = sb("ident_bf", [P, P], BF16)
        upper_bf = sb("upper_bf", [P, P], BF16)
        ones_bf = sb("ones_bf", [P, P], BF16)
        rope = sb("rope", [P, 4, NT, K])
        small = sb("small", [P, C_END])
        wa_sb = sb("wa_sb", [P, 3 * D])
        wqkv_sb = sb("wqkv_sb", [P, QKV])
        wo_sb = sb("wo_sb", [P, NCH, D])
        wmod_sb = sb("wmod_sb", [P, 6 * D])
        rw_sb = sb("rw_sb", [P, E])
        w12_sb = sb("w12_sb", [P, E, 2 * HID])
        w3_sb = sb("w3_sb", [P, E, 2, D])
        qk_bias = sb("qk_bias", [P, 2])
        g1_col = sb("g1_col", [P, 1])
        bv_bc = sb("bv_bc", [P, D])
        g2_bc = sb("g2_bc", [P, D])
        rb_bc = sb("rb_bc", [P, E])

        c_sb = sb("c_sb", [NBATCH, D])
        c_tmp = sb("c_tmp", [NBATCH, 2, D])
        scT = sb("scT", [P, NBATCH])
        modT = sb("modT", [P, 2, NBATCH])
        mod_rows = sb("mod_rows", [NBATCH, 4, D])
        mod_sign = sb("mod_sign", [NBATCH, 2, D])
        mod_mag = sb("mod_mag", [NBATCH, 2, D])
        GA, SB, CB, GB = range(4)
        mod_in = [sb(f"mod_in{k}", [P, 3, D]) for k in range(2)]
        gb_all = sb("gb_all", [P, NBATCH, D])

        x_in = [sb(f"x_in{k}", [P, NT, D]) for k in range(2)]
        stats = sb("stats", [P, NT, 6])
        mv = sb("mv", [P, NT, 2])
        rstd = sb("rstd", [P, NT])
        var_eps = sb("var_eps", [P, NT])
        xn = sb("xn", [P, NT, D])
        hT = sb("hT", [P, T])
        qkA = sb("qkA", [P, 2, T])
        vA = sb("vA", [P, NT, D])
        biasA = sb("biasA", [P, NT])
        sumA = sb("sumA", [P, NT])
        rsumA = sb("rsumA", [P, NT])
        probsA = sb("probsA", [P, 3 * P])
        probsAT = sb("probsAT", [P, 3 * P])
        attA = sb("attA", [P, NT, D])
        stats2 = sb("stats2", [P, NT, 6])
        mv2 = sb("mv2", [P, NT, 2])
        rstd2 = sb("rstd2", [P, NT])
        var2_eps = sb("var2_eps", [P, NT])
        xn2 = sb("xn2", [P, NT, D])
        h2 = sb("h2", [P, NBATCH * NT, D])
        squares = sb("squares", [P, NT, D])
        ms2 = sb("ms2", [P, NT])
        ms2_eps = sb("ms2_eps", [P, NT])
        rms2 = sb("rms2", [P, NT])
        xr = sb("xr", [P, NT, D])
        xrT = sb("xrT", [P, T])
        rope_cos = [sb(f"rope_cos{k}", [P, 512]) for k in range(2)]
        rope_sin = [sb(f"rope_sin{k}", [P, 512]) for k in range(2)]
        qtok = sb("qtok", [P, NT, HQ + HKV, K])
        qT = [sb(f"qT{k}", [P, NCH, T]) for k in range(2)]
        kT = [sb(f"kT{k}", [P, HKV // 2, T]) for k in range(2)]
        vtok = [sb(f"vtok{k}", [P, NT, HKV, K]) for k in range(2)]

        negmax = [sb(f"negmax{k}", [P, 2, 2]) for k in range(2)]
        probs = [sb(f"probs{k}", [P, HKV, T]) for k in range(2)]
        psum_of = [sb(f"psum_of{k}", [P, HKV]) for k in range(2)]
        rden = [sb(f"rden{k}", [P, HKV]) for k in range(2)]
        probsT = [sb(f"probsT{k}", [P, 2 * HKV, P]) for k in range(2)]

        attnT = [sb(f"attnT{k}", [P, NCH, T]) for k in range(2)]

        h = sb("h", [P, NT, D])
        squares3 = sb("squares3", [P, NT, D])
        ms3 = sb("ms3", [P, NT])
        ms3_eps = sb("ms3_eps", [P, NT])
        rms3 = sb("rms3", [P, NT])
        xf = sb("xf", [P, NT, ROW])
        xfT = sb("xfT", [P, T])
        logits = sb("logits", [P, NT, E])
        top8 = sb("top8", [P, NT, E])
        idx8 = sb("idx8", [P, NT, E], U32)
        idxf = sb("idxf", [P, NT, 2])
        gap = sb("gap", [P, NT])
        gap_exp = sb("gap_exp", [P, NT])
        gap_den = sb("gap_den", [P, NT])
        score = sb("score", [P, NT, 2])
        picked = sb("picked", [P, NT, 2, E])
        picked_bf = sb("picked_bf", [P, NT, 2, E], BF16)
        seen_bf = sb("seen_bf", [P, 2, E], BF16)
        kept = sb("kept", [P, NT, 2, E])
        kept_id = sb("kept_id", [P, NT, 2, E])
        kept_any = sb("kept_any", [P, NT, 2])
        kept_expert = sb("kept_expert", [P, NT, 2])
        has = sb("has", [P, NT])
        expert = sb("expert", [P, NT])
        kept_score = sb("kept_score", [P, NT, 2])
        drop_score = sb("drop_score", [P, NT])
        mine = sb("mine", [P, NT, E])
        mine_bf = sb("mine_bf", [P, NT, E], BF16)
        filled_bf = sb("filled_bf", [P, E], BF16)
        rank_of = sb("rank_of", [P, NT, E])
        rank = sb("rank", [P, NT])
        row = sb("row", [P, NT])
        dump_row = sb("dump_row", [P, NT])
        scatter_idx = sb("scatter_idx", [P, NT], U32)
        row_score = sb("row_score", [P, NBLK])
        base_all = sb("base_all", [P, NBATCH * NT, D])
        base_tmp = sb("base_tmp", [P, NT, D])

        xb = [sb(f"xb{k}", [P, ROW]) for k in range(XBUFS)]
        xb_token = [sb(f"xb_token{k}", [P, 1], U32) for k in range(YBUFS)]
        past = sb("past", [P, NBLK])
        result_row = sb("result_row", [P, NBLK], U32)
        xbT = [qT[0][:, 1, k * P:(k + 1) * P] for k in range(2)]
        up = [qT[0][:, 2 + k, :] for k in range(2)]
        prod = [qT[0][:, 4 + k, :] for k in range(2)]
        hid = [qT[0][:, 6 + k, :] for k in range(2)]
        hidT = [qT[1][:, k, :] for k in range(2)]
        yb = [qT[1][:, 2 + k // 2, k % 2 * P:(k % 2 + 1) * P] for k in range(YBUFS)]
        result = [attnT[m // 4][:, m % 4 * OUTS:(m % 4 + 1) * OUTS, :].rearrange("p c (a d) -> p (c a) d", d=D)
                  for m in range(NBATCH // OUTS)]
        zeros = sb("zeros", [P, FILL * ROW])
        blk_need = sb("blk_need", [P, E, E])
        blk_cnt = sb("blk_cnt", [P, E])
        blk_cum = sb("blk_cum", [P, E])
        blk_past = sb("blk_past", [P, NBLK, E])
        blk_pastn = sb("blk_pastn", [P, NBLK, E])
        blk_f = sb("blk_f", [P, 7, NBLK])
        blk_row = sb("blk_row", [P, NBLK], I32)
        blk_expert = sb("blk_expert", [P, NBLK + 2 * XBUFS + 4], I32)

        scores = [[pb(f"scores{k}{half}", [P, 2, T]) for half in range(2)] for k in range(2)]
        tposed = [pb(f"tposed{k}", [P, 512]) for k in range(2)]
        shared = [pb(f"shared{k}", [P, 512]) for k in range(2)]

        s_first = sem("first_loaded")
        s_const = sem("const_loaded")
        s_wa, s_wf, s_wt = sem("a_weights_loaded"), sem("f_weights_loaded"), sem("t_weights_loaded")
        s_moew = sem("expert_weights_loaded")
        s_modout = sem("mod_rows_stored")
        s_mod = [sem(f"mod_loaded{k}") for k in range(2)]
        s_gb = sem("gb_loaded")
        s_x = [sem(f"x_loaded{k}") for k in range(2)]
        s_zeroed = sem("tables_zeroed")
        s_zeros = sem("zeros_ready")
        s_setup_act = sem("setup_act")
        s_setup_dve = sem("setup_dve")
        s_setup_pe = sem("setup_pe")
        s_full = [sem(f"shared_full{k}") for k in range(2)]
        s_free = [sem(f"shared_free{k}") for k in range(2)]
        s_scores = sem("scores_full")
        s_negmax = sem("negmax_ready")
        s_exps = sem("exponentials_ready")
        s_rden = sem("rden_ready")
        s_probs = sem("probs_ready")
        s_tfull = sem("tposed_full")
        s_tfree = sem("tposed_free")
        s_vtok = sem("vtok_ready")
        s_var = sem("var_ready")
        s_rstd = sem("rstd_ready")
        s_xn = sem("xn_ready")
        s_biasA = sem("biasA_ready")
        s_var2 = sem("var2_ready")
        s_rstd2 = sem("rstd2_ready")
        s_x2 = sem("x2_done")
        s_h2 = sem("h2_ready")
        s_ms2 = sem("ms2_ready")
        s_rms2 = sem("rms2_ready")
        s_xr = sem("xr_ready")
        s_roped = sem("roped")
        s_ms3 = sem("ms3_ready")
        s_rms3 = sem("rms3_ready")
        s_xf = sem("xf_ready")
        s_gap = sem("gap_ready")
        s_gexp = sem("gap_exp_ready")
        s_picked = sem("picked_ready")
        s_mine = sem("mine_ready")
        s_sidx = sem("scatter_idx_ready")
        s_score = sem("score_ready")
        s_scat = sem("rows_scattered")
        s_dfront = sem("dve_front_chain")
        s_dtail = sem("dve_tail_chain")
        s_vareps, s_var2eps = sem("var_eps_ready"), sem("var2_eps_ready")
        s_ms2eps, s_ms3eps = sem("ms2_eps_ready"), sem("ms3_eps_ready")
        s_filled = sem("filled_ready")
        s_dstats = sem("dve_stats_chain")
        s_dend = sem("dve_end_chain")
        s_tab = sem("block_table_ready")
        s_total = sem("totals_ready")
        s_xb = [sem(f"xb_loaded{k}") for k in range(XBUFS)]
        s_xbTp = sem("xb_transposed")
        s_xbT = sem("xbT_ready")
        s_up = sem("up_products")
        s_upc = sem("up_copied")
        s_prod = sem("prod_ready")
        s_hid = sem("hid_ready")
        s_hTp = sem("hid_transposed")
        s_hT = sem("hidT_ready")
        s_yp = sem("y_product")
        s_yb = sem("yb_ready")
        s_ys = [sem(f"y_stored{k}") for k in range(YBUFS)]
        s_past = sem("past_ready")
        s_token = sem("result_row_ready")
        s_idx = sem("xb_token_ready")
        s_yl = [sem(f"results_loaded{m}") for m in range(NBATCH // OUTS)]
        s_scaled = sem("y_scaled")
        s_yo = sem("yo_ready")
        s_scaled_pool, s_yo_pool = sem("y_scaled_pool"), sem("yo_ready_pool")
        s_out = sem("out_stored")

        CONSTS = (s_first, 2 * 16)
        iota8 = small[:, C_IOTA8:C_IOTA8 + E]
        block = ctx.enter_context(nc.Block())

        def later_weights(eng, b):
            if isinstance(b, int) and b == -1:
                eng.wait_ge(s_wf, LOADED_F)
            if isinstance(b, int) and b == 1:
                eng.wait_ge(s_wt, LOADED_T)

        def finish(eng, ops, mine):
            tiles = OUTS * NT
            for n, m in enumerate(mine):
                scaled, ready = (s_scaled, s_yo) if eng is nc.vector else (s_scaled_pool, s_yo_pool)
                eng.wait_ge(s_yl[m], 16)
                y = result[m].rearrange("p (b i) d -> p b i d", b=OUTS)
                ops.tensor_tensor(y, y, gb_all[:, OUTS * m:OUTS * (m + 1), :].unsqueeze(2).to_broadcast(
                    [P, OUTS, NT, D]), ALU.mult).then_inc(scaled, 1)
                eng.wait_ge(scaled, n + 1)
                ops.tensor_tensor(result[m], result[m], base_all[:, tiles * m:tiles * (m + 1), :], ALU.add
                                  ).then_inc(ready, 1)

        @block.sync
        def _(sp):
            def load_x(n, k):
                sp.dma_start(x_in[k][:, :, :], x[n, :, :].rearrange("(i p) d -> p i d", p=P)
                             if isinstance(n, int) else
                             x[bass.ds(n, 1), :, :].rearrange("b (i p) d -> p (b i) d", p=P)).then_inc(s_x[k], 16)

            def load_mod(n, k):
                sp.dma_start(mod_in[k][:, :, :], mod_dram[span(n, 1), 0:GB * D].rearrange("a (j d) -> a j d", j=GB)
                             .to_broadcast([P, GB, D])).then_inc(s_mod[k], 16)

            sp.dma_start(c_sb[:, :], c).then_inc(s_first, 16)
            sp.dma_start(ident[:, :], k_ident).then_inc(s_first, 16)
            load_x(0, 0)
            sp.dma_start(small[:, :], k_small).then_inc(s_const, 16)
            sp.dma_start(wmod_sb[:, :], wmod).then_inc(s_const, 16)
            sp.dma_start(stage_f32[:, 0, :], k_mask).then_inc(s_const, 16)
            sp.dma_start(stage_f32[:, 1, :], k_upper).then_inc(s_const, 16)
            sp.dma_start(wa_sb[:, :], W).then_inc(s_wa, 16)
            sp.dma_start(qk_bias[:, :], bias[0:2 * D].rearrange("(j p) -> p j", p=P),
                         allow_slow_non_contiguous=True).then_inc(s_wa, 16)
            sp.dma_start(bv_bc[:, :], bias[2 * D:3 * D].rearrange("(a d) -> a d", a=1).to_broadcast([P, D])
                         ).then_inc(s_wa, 16)
            load_x(1, 1)
            sp.dma_start(g1_col[:, :], g1.rearrange("(p a) -> p a", a=1)).then_inc(s_wf, 16)
            sp.dma_start(wqkv_sb[:, HQ * K:(HQ + HKV) * K], wk).then_inc(s_wf, 16)
            sp.dma_start(wqkv_sb[:, (HQ + HKV) * K:], wv).then_inc(s_wf, 16)
            sp.dma_start(rope[:, :, :, :], k_rope).then_inc(s_wf, 16)
            sp.dma_start(wqkv_sb[:, 0:HQ * K], wq).then_inc(s_wf, 16)
            sp.wait_ge(s_setup_dve, SETUP_MOD)
            sp.dma_start(mod_dram, mod_rows[:, :, :].rearrange("b j d -> b (j d)")).then_inc(s_modout, 16)
            sp.wait_ge(s_modout, 16)
            for n in range(2):
                load_mod(n, n)
            sp.dma_start(gb_all[:, :, :], mod_dram[:, GB * D:].unsqueeze(0).to_broadcast([P, NBATCH, D])
                         ).then_inc(s_gb, 16)
            sp.dma_start(g2_bc[:, :], g2.rearrange("(a d) -> a d", a=1).to_broadcast([P, D])).then_inc(s_wt, 16)
            sp.dma_start(rb_bc[:, :], router_b.rearrange("(a d) -> a d", a=1).to_broadcast([P, E])
                         ).then_inc(s_wt, 16)
            sp.dma_start(rw_sb[:, :], router_w).then_inc(s_wt, 16)
            sp.dma_start(wo_sb[:, :, :], wo.rearrange("(c p) d -> p c d", p=P)).then_inc(s_wt, 16)
            sp.wait_ge(s_zeros, 1)
            for rows in (xs_dram[0:DUMP, :], ys_dram[0:NTOK, :]):
                width = rows.shape[1] * FILL
                sp.dma_start(rows.rearrange("(n p r) d -> p n (r d)", p=P, r=FILL),
                             zeros[:, 0:width].unsqueeze(1).to_broadcast([P, rows.shape[0] // P // FILL, width])
                             ).then_inc(s_zeroed, 16)
            sp.dma_start(xs_dram[SPARE:SPARE + P, :], zeros[:, 0:ROW]).then_inc(s_zeroed, 16)
            for e in range(E):
                sp.dma_start(w12_sb[:, e, 0:HID], w1[e]).then_inc(s_moew, 16)
                sp.dma_start(w12_sb[:, e, HID:], w2[e]).then_inc(s_moew, 16)
                sp.dma_start(w3_sb[:, e, :, :], w3[e].rearrange("(c p) d -> p c d", p=P)).then_inc(s_moew, 16)
            with sp.Fori(2, NBATCH - 1, 2) as n:
                for k in range(2):
                    sp.wait_ge(s_h2, n + (k - 1))
                    load_x(n + k, k)
                    load_mod(n + k, k)

            sp.wait_ge(s_tab, 1)
            sp.wait_ge(s_scat, 16 * NBATCH * NT)

            def load_block(j, k):
                r = sp.value_load(blk_row[0:1, bass.ds(j, 1)], min_val=0, max_val=SPARE)
                sp.dma_start(xb[k][:, :], xs_dram[bass.ds(r, P), :]).then_inc(s_xb[k], 16)

            for j in range(XBUFS):
                load_block(j, j)
            with sp.Fori(XBUFS, NBLK - XBUFS + 1, XBUFS) as j:
                for k in range(XBUFS):
                    sp.wait_ge(s_xbTp, j + (k + 1 - XBUFS))
                    sp.wait_ge(s_token, j + (k + 1 - XBUFS))
                    load_block(j + k, k)

            for k in range(YBUFS):
                sp.wait_ge(s_ys[k], 16 * NBLK // YBUFS)

            for m in range(NBATCH // OUTS):
                sp.dma_start(result[m], ys_dram[m * OUTS * T:(m + 1) * OUTS * T, :].rearrange("(i p) d -> p i d", p=P)
                             ).then_inc(s_yl[m], 16)

        @block.tensor
        def _(pe):
            mm, tr = nc.tensor.matmul, nc.tensor.transpose

            pe.wait_ge(s_first, 2 * 16)
            pe.wait_ge(s_setup_dve, SETUP_SILU)
            tr(shared[0][:, 0:NBATCH], c_tmp[:, 1, :], ident[0:NBATCH, 0:NBATCH]).then_inc(s_setup_pe, 1)
            pe.wait_ge(s_setup_dve, SETUP_SCT)
            pe.wait_ge(s_const, 4 * 16)
            mm(shared[1][0:NBATCH, :], scT[:, :], wmod_sb[:, 2 * D:6 * D], start=True, stop=True
               ).then_inc(s_setup_pe, 1)
            for j in range(2):
                last = mm(shared[0][:, j * NBATCH:(j + 1) * NBATCH], wmod_sb[:, j * D:(j + 1) * D], scT[:, :],
                          start=True, stop=True)
            last.then_inc(s_setup_pe, 1)
            pe.wait_ge(s_setup_dve, SETUP_ALL)
            pe.wait_ge(s_wa, LOADED_A)

            def evacuated(stages, b, into=None):
                for bank in range(2):
                    of_bank = [s for s in stages if BANK[s] == bank]
                    if of_bank and (into is None or bank != BANK[into]):
                        pe.wait_ge(s_free[bank], uses_before(of_bank[-1], b) + 1)

            def scores_of(u, n, k):
                i, g = QUADS[u]
                wait(pe, s_exps, 8 * n + (u - 1))
                nk = (i + 1) * P
                banks = scores[u % 2]
                for half in range(2):
                    mm(banks[half][:, :, i * P:(i + 1) * P], ident_bf[:, :],
                       mask_bf[:, :].unsqueeze(1).to_broadcast([P, 2, P]), start=True, stop=False,
                       skip_group_check=True)
                for kv in range(HKV):
                    half, rows = kv % 2, slice(K * (kv % 2), K * (kv % 2) + K)
                    last = mm(banks[half][:, kv // 2, 0:nk], qT[k][rows, 2 * g + kv // 2, i * P:(i + 1) * P],
                              kT[k][rows, kv // 2, 0:nk], start=False, stop=True, skip_group_check=True)
                last.then_inc(s_scores, 1)

            def body(b, k):
                later_weights(pe, b)
                t_used = 0
                for kind, what in stages_of(b):
                    if kind == "scores":
                        u = what % 8
                        if u < 2:
                            ahead = 1 if what >= 8 else 0
                            evacuated(("f_k0T", "f_q00T") if u == 0 else ("f_k1T", "f_q10T"), b - 1 + ahead)
                            scores_of(u, b + ahead, 1 - k if ahead else k)
                        else:
                            if u in (4, 5):
                                evacuated(["f_q01T" if u == 4 else "f_q11T"], b - 1)
                            scores_of(u, b, k)
                        continue
                    if kind == "transpose":
                        u = what
                        i, g = QUADS[u]
                        pe.wait_ge(s_probs, 8 * b + (u + 1))
                        blocks = [(kv, kt) for kv in range(HKV) for kt in range(i + 1)]
                        for at in range(0, len(blocks), 4):
                            wait(pe, s_tfree, 12 * b + (t_used - 1))
                            for m, (kv, kt) in enumerate(blocks[at:at + 4]):
                                last = tr(tposed[t_used % 2][:, m * P:(m + 1) * P],
                                          probs[u % 2][:, kv, kt * P:(kt + 1) * P], ident[:, :])
                            last.then_inc(s_tfull, 1)
                            t_used += 1
                        continue
                    stage = f"pv{what}" if kind == "values" else what
                    if kind in ("max", "exps", "normalize") or stage in NO_BANK:
                        continue
                    bank = shared[BANK[stage]]
                    wait(pe, s_free[BANK[stage]], uses_before(stage, b))
                    if kind == "values":
                        i, g = QUADS[what]
                        pe.wait_ge(s_tfree, 12 * b + transposes_to(what + 1))
                        if what < 2:
                            pe.wait_ge(s_vtok, 2 * b + (what + 1))
                        for kv in range(HKV):
                            half = slice(K * (kv % 2), K * (kv % 2) + K)
                            for kt in range(i + 1):
                                last = mm(bank[half, kv // 2 * P:(kv // 2 + 1) * P], vtok[k][:, kt, kv, :],
                                          probsT[what % 2][:, kv * (i + 1) + kt, :], start=kt == 0, stop=kt == i)
                    elif stage == "a_xnT":
                        pe.wait_ge(s_xn, b + 3)
                        for i in range(NT):
                            last = tr(bank[:, i * P:(i + 1) * P], xn[:, i, :], ident[:, :])
                    elif stage == "a_qk":
                        evacuated(["a_xnT"], b, into=stage)
                        for j in range(2):
                            last = mm(bank[:, j * T:(j + 1) * T], wa_sb[:, j * D:(j + 1) * D], hT[:, :],
                                      start=True, stop=True)
                    elif stage == "a_va":
                        for i in range(NT):
                            last = mm(bank[:, i * P:(i + 1) * P], hT[:, i * P:(i + 1) * P],
                                      wa_sb[:, 2 * D:3 * D], start=True, stop=True)
                    elif stage == "a_sa":
                        evacuated(["a_qk"], b, into=stage)
                        for i in range(NT):
                            mm(bank[:, 2 * i * P:(2 * i + 1) * P], ident_bf[:, :], mask_bf[:, :],
                               start=True, stop=False, skip_group_check=True)
                            last = mm(bank[:, i * P:(2 * i + 1) * P], qkA[:, 0, i * P:(i + 1) * P],
                                      qkA[:, 1, 0:(i + 1) * P], start=False, stop=True, skip_group_check=True)
                    elif stage == "a_ta":
                        evacuated(["a_sa"], b, into=stage)
                        for j in range(3):
                            last = tr(bank[:, j * P:(j + 1) * P], probsA[:, j * P:(j + 1) * P], ident[:, :])
                    elif stage == "a_pva":
                        evacuated(["a_va", "a_ta"], b, into=stage)
                        mm(bank[:, 0:P], probsAT[:, 0:P], vA[:, 0, :], start=True, stop=True)
                        mm(bank[:, P:2 * P], probsAT[:, P:2 * P], vA[:, 0, :], start=True, stop=False)
                        last = mm(bank[:, P:2 * P], probsAT[:, 2 * P:3 * P], vA[:, 1, :], start=False, stop=True)
                    elif stage == "f_xrT":
                        pe.wait_ge(s_xr, b + 2)
                        for i in range(NT):
                            last = tr(bank[:, i * P:(i + 1) * P], xr[:, i, :], ident[:, :])
                    elif stage.startswith("f_p"):
                        evacuated(["f_xrT"], b, into=stage)
                        i, j = int(stage[3]), "abk".index(stage[4])
                        last = mm(bank[:, :], xrT[:, i * P:(i + 1) * P], wqkv_sb[:, j * 512:(j + 1) * 512],
                                  start=True, stop=True)
                    elif stage.startswith("f_k") or stage.startswith("f_q"):
                        i = int(stage[3])
                        first, count = (HQ // 2, 2) if stage[2] == "k" else (4 * int(stage[4]), 4)
                        done = 1 if stage[2] == "k" else 2 + int(stage[4])
                        pe.wait_ge(s_roped, 6 * b + (6 + 3 * i + done))
                        for m in range(count):
                            last = tr(bank[:, m * P:(m + 1) * P],
                                      qtok[:, i, 2 * (first + m):2 * (first + m) + 2, :]
                                      .rearrange("p h d -> p (h d)"), ident[:, :])
                    elif stage in ("t_wo0", "t_wo1"):
                        i = int(stage[4])
                        evacuated([f"pv{6 + i}"], b - 1, into=stage)
                        for ch in range(NCH):
                            last = mm(bank[:, 0:D], attnT[1 - k][:, ch, i * P:(i + 1) * P], wo_sb[:, ch, :],
                                      start=ch == 0, stop=ch == NCH - 1)
                    elif stage == "t_xfT":
                        pe.wait_ge(s_xf, b)
                        for i in range(NT):
                            last = tr(bank[:, i * P:(i + 1) * P], xf[:, i, 0:D], ident[:, :])
                    elif stage == "t_logits":
                        evacuated(["t_xfT"], b, into=stage)
                        for i in range(NT):
                            last = mm(bank[:, i * E:(i + 1) * E], xfT[:, i * P:(i + 1) * P], rw_sb[:, :],
                                      start=True, stop=True)
                    else:
                        pick, seen, w = ((picked_bf, seen_bf, 2 * E) if stage == "t_cum" else
                                         (mine_bf, filled_bf, E))
                        pe.wait_ge(s_picked if stage == "t_cum" else s_mine, b)
                        flat = "p a e -> p (a e)"
                        seen_all = seen[:, :, :].rearrange(flat) if stage == "t_cum" else seen[:, :]
                        for i in range(NT):
                            o = bank[:, i * w:(i + 1) * w]
                            of = [pick[:, m].rearrange(flat) if stage == "t_cum" else pick[:, m, :]
                                  for m in range(i + 1)]
                            mm(o, ones_bf[:, :], seen_all, start=True, stop=False)
                            for m in range(i):
                                mm(o, ones_bf[:, :], of[m], start=False, stop=False)
                            last = mm(o, upper_bf[:, :], of[i], start=False, stop=True)
                    last.then_inc(s_full[BANK[stage]], 1)

            bodies(pe, body)

            pe.wait_ge(s_filled, NBATCH)
            pe.wait_ge(s_tfree, 12 * NBATCH)
            mm(tposed[0][:, 0:E], ones_bf[:, :], filled_bf[:, :], start=True, stop=True).then_inc(s_total, 1)
            pe.wait_ge(s_tab, 1)
            pe.wait_ge(s_moew, 16 * 3 * E)

            def x_transpose(t, k):
                pe.wait_ge(s_xb[k % XBUFS], 16 // XBUFS * t + (16 - 16 // XBUFS * (k % XBUFS)))
                wait(pe, s_xbT, t - 1)
                tr(scores[0][k % 2][:, 0, 0:P], xb[k % XBUFS][:, 0:D], ident[:, :]).then_inc(s_xbTp, 1)

            experts = []

            def load_experts(t):
                regs = [pe.alloc_register(f"expert{len(experts)}_{m}") for m in range(2 * XBUFS)]
                pe.load(regs, blk_expert[0:1, span(t, 2 * XBUFS)])
                experts.append([pe.snap(r, min_val=0, max_val=E - 1) for r in regs])


            def go_up(t, k, e):
                pe.wait_ge(s_xbT, t + 1)
                wait(pe, s_prod, t - 1)
                mm(scores[1][k % 2][:, :, :].rearrange("p a b -> p (a b)"), xbT[k % 2],
                   w12_sb[:, bass.ds(e, 1), :].rearrange("p a n -> p (a n)"), start=True, stop=True
                   ).then_inc(s_up, 1)

            def hid_transpose(t, k):
                pe.wait_ge(s_hid, t + 1)
                wait(pe, s_hT, t - 1)
                for m in range(2):
                    last = tr(tposed[k % 2][:, m * P:(m + 1) * P], hid[k % 2][:, m * P:(m + 1) * P], ident[:, :])
                last.then_inc(s_hTp, 1)

            def come_down(t, k, e):
                pe.wait_ge(s_hT, t + 1)
                wait(pe, s_yb, t - 1)
                for m in range(2):
                    last = mm(shared[k % 2][:, 0:D], hidT[k % 2][:, m * P:(m + 1) * P],
                              w3_sb[:, bass.ds(e, 1), m, :].rearrange("p a d -> p (a d)"),
                              start=m == 0, stop=m == 1)
                last.then_inc(s_yp, 1)

            def step(t, k):
                if k == 0:
                    load_experts(t)
                if has_block(t, 4):
                    hid_transpose(t - 4, k)
                if has_block(t, 5):
                    come_down(t - 5, k - 5, experts[-1][k])
                if has_block(t, 0):
                    x_transpose(t, k)
                if has_block(t, 1):
                    go_up(t - 1, k - 1, experts[-1][k + 4])

            steps(pe, step)

        @block.scalar
        def _(act):
            act.wait_ge(s_first, 2 * 16)
            nc.scalar.activation(c_tmp[:, 0, :], c_sb[:, :], ACT.Exp, scale=-1.0).then_inc(s_setup_act, 1)
            act.wait_ge(s_wa, LOADED_A)
            act.wait_ge(s_setup_dve, SETUP_ALL)

            def copied(ins, stage):
                ins.then_inc(s_free[BANK[stage]], 1)

            def exps(u, n):
                i, g = QUADS[u]
                act.wait_ge(s_negmax, 8 * n + (u + 1))
                t_before = sum(QUADS[m][0] + 1 for m in range(u - 1)) if u else -(QUADS[7][0] + 1)
                wait(act, s_tfull, 12 * n + t_before)
                for kv in range(HKV):
                    last = nc.scalar.activation(
                        probs[u % 2][:, kv, 0:(i + 1) * P], scores[u % 2][kv % 2][:, kv // 2, 0:(i + 1) * P],
                        ACT.Exp, bias=negmax[u % 2][:, kv % 2, kv // 2:kv // 2 + 1],
                        accum_out=psum_of[u % 2][:, kv:kv + 1])
                last.then_inc(s_exps, 1)

            def body(b, k):
                na, nf, nk = b + 2, b + 1, 1 - k
                later_weights(act, b)
                t_used = 0
                for kind, what in stages_of(b):
                    if kind == "exps":
                        exps(what % 8, b if what < 8 else b + 1)
                        continue
                    if kind == "transpose":
                        i, g = QUADS[what]
                        for at in range(i + 1):
                            act.wait_ge(s_tfull, 12 * b + (t_used + 1))
                            nc.scalar.copy(probsT[what % 2][:, 4 * at:4 * at + 4, :].rearrange("p m q -> p (m q)"),
                                           tposed[t_used % 2][:, :]).then_inc(s_tfree, 1)
                            t_used += 1
                        continue
                    if kind != "stage":
                        continue
                    stage = what

                    def full():
                        act.wait_ge(s_full[BANK[stage]], uses_before(stage, b) + 1)

                    bank = shared[BANK["a_sa" if stage == "a_ea" else stage]] if (
                        stage == "a_ea" or stage not in NO_BANK) else None
                    if stage == "a_xnT":
                        full()
                        sl = span(na, 1)
                        copied(nc.scalar.activation(hT[:, :], bank[:, 0:T], ACT.Identity,
                                                    bias=modT[:, 0, sl], scale=modT[:, 1, sl]), stage)
                    elif stage == "a_qk":
                        full()
                        for j in range(2):
                            last = nc.scalar.activation(qkA[:, j, :], bank[:, j * T:(j + 1) * T], ACT.Identity,
                                                        bias=qk_bias[:, j:j + 1])
                        copied(last, stage)
                    elif stage == "a_ea":
                        act.wait_ge(s_biasA, na + 1)
                        for i in range(NT):
                            last = nc.scalar.activation(probsA[:, i * P:(2 * i + 1) * P],
                                                        bank[:, i * P:(2 * i + 1) * P], ACT.Exp,
                                                        bias=biasA[:, i:i + 1], scale=D ** -0.5,
                                                        accum_out=sumA[:, i:i + 1])
                        copied(last, "a_sa")
                    elif stage == "a_ta":
                        full()
                        copied(nc.scalar.copy(probsAT[:, :], bank[:, 0:3 * P]), stage)
                    elif stage == "f_xrT":
                        full()
                        copied(nc.scalar.activation(xrT[:, :], bank[:, 0:T], ACT.Identity, scale=g1_col[:, 0:1]),
                               stage)
                    elif stage[0:3] in ("f_k", "f_q"):
                        full()
                        i = int(stage[3])
                        if stage[2] == "k":
                            dst, m = kT[nk][:, :, i * P:(i + 1) * P], 2
                        else:
                            part4 = int(stage[4])
                            dst, m = qT[nk][:, 4 * part4:4 * part4 + 4, i * P:(i + 1) * P], 4
                        copied(nc.scalar.copy(dst, bank[:, 0:m * P].rearrange("p (m q) -> p m q", m=m)), stage)
                    elif stage == "t_xfT":
                        full()
                        copied(nc.scalar.copy(xfT[:, :], bank[:, 0:T]), stage)
                    elif stage == "t_gexp":
                        act.wait_ge(s_gap, b)
                        nc.scalar.activation(gap_exp[:, :], gap[:, :], ACT.Exp).then_inc(s_gexp, 1)

            bodies(act, body)

            def step(t, k):
                if has_block(t, 0):
                    act.wait_ge(s_xbTp, t + 1)
                    wait(act, s_up, t - 1)
                    nc.scalar.copy(xbT[k % 2], scores[0][k % 2][:, 0, 0:P]).then_inc(s_xbT, 1)
                if has_block(t, 3):
                    act.wait_ge(s_prod, t - 2)
                    wait(act, s_hTp, t - 4)
                    nc.scalar.activation(hid[(k + 1) % 2], prod[(k + 1) % 2], ACT.Gelu).then_inc(s_hid, 1)
                if has_block(t, 1):
                    act.wait_ge(s_up, t)
                    wait(act, s_prod, t - 2)
                    nc.scalar.copy(up[(k + 1) % 2], scores[1][(k + 1) % 2][:, 0, :]).then_inc(s_upc, 1)

            act.wait_ge(s_tab, 1)
            steps(act, step)

            for m in range(NBATCH // OUTS):
                before = [n for n in range(m + 1) if (n in POOL_OUTS) == (m in POOL_OUTS)]
                act.wait_ge(s_yo_pool if m in POOL_OUTS else s_yo, len(before))
                act.dma_start(out[m * OUTS:(m + 1) * OUTS, :, :].rearrange("b (i p) d -> p (b i) d", p=P), result[m]
                              ).then_inc(s_out, 16)
            act.wait_ge(s_out, 16 * NBATCH // OUTS)

        @block.gpsimd
        def _(pool):
            half = small[:, C_HALF:C_HALF + NT]
            pool.wait_ge(s_const, 4 * 16)
            nc.gpsimd.memset(zeros[:, :], 0.0).then_inc(s_zeros, 1)

            def rsqrt(dst, tmp, src, scale, eps, sem_in, value, sem_mid, sem_out):
                wait_alone(pool, sem_in, value, CONSTS)
                nc.gpsimd.tensor_scalar(tmp, src, scale, eps, ALU.mult, ALU.add).then_inc(sem_mid, 1)
                pool.wait_ge(sem_mid, value)
                nc.gpsimd.tensor_tensor(dst, tmp, half, ALU.pow).then_inc(sem_out, 1)

            def body(b, k):
                na = b + 2
                for kind, what in stages_of(b):
                    if kind == "normalize":
                        m, u = (b if what < 8 else b + 1), what % 8
                        some = probs[u % 2][:, :, 0:(QUADS[u][0] + 1) * P]
                        pool.wait_ge(s_rden, 8 * m + (u + 1))
                        nc.gpsimd.tensor_tensor(some, some, rden[u % 2][:, :].unsqueeze(2).to_broadcast(
                            [P, HKV, (QUADS[u][0] + 1) * P]), ALU.mult).then_inc(s_probs, 1)
                        continue
                    if kind != "stage":
                        continue
                    stage = what
                    if stage == "a_rstd":
                        rsqrt(rstd[:, :], var_eps[:, :], mv[:, :, 1], 1.0, 1e-5, s_var, na + 1, s_vareps, s_rstd)
                    elif stage == "a_rstd2":
                        rsqrt(rstd2[:, :], var2_eps[:, :], mv2[:, :, 1], 1.0, 1e-5, s_var2, na + 1, s_var2eps,
                              s_rstd2)
                    elif stage == "a_rms":
                        rsqrt(rms2[:, :], ms2_eps[:, :], ms2[:, :], 1.0 / D, 1e-6, s_ms2, na + 1, s_ms2eps,
                              s_rms2)
                    elif stage.startswith("f_r"):
                        product = "f_p" + stage[3:]
                        i, j = int(stage[3]), "kab".index(stage[4])
                        m = 3 * i + j
                        heads = (HQ, HKV) if j == 0 else (8 * (j - 1), 8)
                        pool.wait_ge(s_free[BANK[product]], uses_before(product, b) + 1)
                        src = slice(0, heads[1] * K)
                        nc.gpsimd.tensor_tensor(
                            qtok[:, i, heads[0]:heads[0] + heads[1], :].rearrange("p h d -> p (h d)"),
                            rope_cos[m % 2][:, src], rope_sin[m % 2][:, src], ALU.add).then_inc(s_roped, 1)
                    elif stage == "t_rms":
                        rsqrt(rms3[:, :], ms3_eps[:, :], ms3[:, :], 1.0 / D, 1e-6, s_ms3, b, s_ms3eps, s_rms3)
                    elif stage == "t_send":
                        if isinstance(b, int) and b == 1:
                            pool.wait_ge(s_zeroed, ZEROED)
                        wait_alone(pool, s_sidx, b, CONSTS)
                        wait_alone(pool, s_score, b, CONSTS)
                        for i in range(NT):
                            nc.gpsimd.indirect_dma_start(
                                out=xs_dram, out_offset=bass.IndirectOffsetOnAxis(ap=scatter_idx[:, i:i + 1], axis=0),
                                in_=xf[:, i, :], in_offset=None).then_inc(s_scat, 16)

            bodies(pool, body)

            def step(t, k):
                if has_block(t, 6):
                    j, k = t - 6, (k - 6) % YBUFS
                    wait_alone(pool, s_token, j + 1, CONSTS)
                    if not isinstance(j, int) or j >= YBUFS:
                        wait_alone(pool, s_ys[k], 16 // YBUFS * j - 16 // YBUFS * k, CONSTS)
                    nc.gpsimd.tensor_copy(xb_token[k][:, :], result_row[:, span(j, 1)]).then_inc(s_idx, 1)
                    wait_alone(pool, s_idx, j + 1, CONSTS)
                    wait_alone(pool, s_yb, j + 1, CONSTS)
                    nc.gpsimd.indirect_dma_start(
                        out=ys_dram, out_offset=bass.IndirectOffsetOnAxis(ap=xb_token[k][:, 0:1], axis=0),
                        in_=yb[k], in_offset=None).then_inc(s_ys[k], 16)

            steps(pool, step)
            finish(pool, nc.gpsimd, POOL_OUTS)

        @block.vector
        def _(dve):
            v = nc.vector
            tt, ts, stt = v.tensor_tensor, v.tensor_scalar, v.scalar_tensor_tensor
            count = {}

            def link(ins, sem_, base=0, alone=False):
                ins.then_inc(sem_, 1)
                count[id(sem_)] = count.get(id(sem_), 0) + 1
                if alone:
                    wait_alone(dve, sem_, base + count[id(sem_)], CONSTS)
                else:
                    dve.wait_ge(sem_, base + count[id(sem_)])

            v.memset(ones_bf[:, :], 1.0)
            v.memset(seen_bf[:, :, :], 0.0)
            v.memset(filled_bf[:, :], 0.0)
            v.memset(xf[:, :, D:ROW], 0.0)
            v.memset(blk_expert[:, :], 0)

            def row_statistics(n, k):
                wait_alone(dve, s_x[k], 8 * n + (16 - 8 * k), CONSTS)
                for i in range(NT):
                    last = v.bn_stats(stats[:, i, :], x_in[k][:, i, :])
                link(last, s_dstats, STATS_LINKS * n, alone=True)
                for i in range(NT):
                    last = v.bn_aggr(mv[:, i, :], stats[:, i, :])
                last.then_inc(s_var, 1)

            dve.wait_ge(s_setup_act, 1)
            link(ts(c_tmp[:, 1, :], c_tmp[:, 0, :], 1.0, None, ALU.add), s_setup_dve)
            link(v.reciprocal(c_tmp[:, 0, :], c_tmp[:, 1, :]), s_setup_dve)
            link(tt(c_tmp[:, 1, :], c_tmp[:, 0, :], c_sb[:, :], ALU.mult), s_setup_dve)
            row_statistics(0, 0)
            dve.wait_ge(s_setup_pe, 1)
            link(v.tensor_copy(scT[:, :], shared[0][:, 0:NBATCH]), s_setup_dve)
            dve.wait_ge(s_setup_pe, 2)
            mod_ps = shared[1][0:NBATCH, :].rearrange("b (j d) -> b j d", j=4)
            v.tensor_copy(mod_rows[:, SB, :], mod_ps[:, 1, :])
            ts(mod_rows[:, CB, :], mod_ps[:, 2, :], 1.0, None, ALU.add)
            gates = mod_ps[:, 0:4:3, :]
            link(ts(mod_sign[:, :, :], gates, 0.0, 2.0, ALU.is_ge, ALU.mult), s_setup_dve)
            link(ts(mod_sign[:, :, :], mod_sign[:, :, :], 1.0, None, ALU.subtract), s_setup_dve)
            link(tt(mod_mag[:, :, :], gates, mod_sign[:, :, :], ALU.mult), s_setup_dve)
            link(stt(mod_rows[:, 0:4:3, :], mod_mag[:, :, :], 0.25, mod_sign[:, :, :], ALU.max, ALU.mult),
                 s_setup_dve)
            dve.wait_ge(s_setup_pe, 3)
            v.tensor_copy(modT[:, 0, :], shared[0][:, 0:NBATCH])
            link(ts(modT[:, 1, :], shared[0][:, NBATCH:2 * NBATCH], 1.0, None, ALU.add), s_setup_dve)
            assert count[id(s_setup_dve)] == SETUP_ALL
            dve.wait_ge(s_const, 4 * 16)
            v.tensor_copy(mask_bf[:, :], stage_f32[:, 0, :])
            v.tensor_copy(upper_bf[:, :], stage_f32[:, 1, :])
            v.tensor_copy(ident_bf[:, :], ident[:, :])
            dve.wait_ge(s_wa, LOADED_A)

            def copied(ins, stage):
                ins.then_inc(s_free[BANK[stage]], 1)

            def norm(dst, src, mv_, rstd_):
                for i in range(NT):
                    last = ts(dst[:, i, :], src(i), mv_[:, i, 0:1], rstd_[:, i:i + 1], ALU.subtract, ALU.mult)
                return last

            def block_table():
                def elink(ins):
                    link(ins, s_dend)

                dve.wait_ge(s_total, 1)
                thr = small[:, C_THR:C_THR + E * E].rearrange("p (e k) -> p e k", e=E)
                lower = small[:, C_LOWER:C_LOWER + E * E].rearrange("p (e f) -> p e f", e=E)
                number = small[:, C_BLK:C_BLK + NBLK]
                elink(tt(blk_need[:, :, :], tposed[0][:, 0:E].unsqueeze(2).to_broadcast([P, E, E]), thr, ALU.is_gt))
                elink(v.tensor_reduce(blk_cnt[:, :], blk_need[:, :, :], AX_X, ALU.add))
                elink(tt(blk_need[:, :, :], lower, blk_cnt[:, :].unsqueeze(1).to_broadcast([P, E, E]), ALU.mult))
                elink(v.tensor_reduce(blk_cum[:, :], blk_need[:, :, :], AX_X, ALU.add))
                elink(tt(blk_past[:, :, :], blk_cum[:, :].unsqueeze(1).to_broadcast([P, NBLK, E]),
                         number.unsqueeze(2).to_broadcast([P, NBLK, E]), ALU.is_le))
                v.tensor_reduce(blk_f[:, 0, :], blk_past[:, :, :], AX_X, ALU.add)
                elink(tt(blk_pastn[:, :, :], blk_past[:, :, :], blk_cnt[:, :].unsqueeze(1).to_broadcast([P, NBLK, E]),
                         ALU.mult))
                elink(v.tensor_reduce(blk_f[:, 1, :], blk_pastn[:, :, :], AX_X, ALU.add))
                ts(blk_f[:, 2, :], blk_f[:, 0, :], float(E), None, ALU.is_lt)
                elink(tt(blk_f[:, 3, :], number, blk_f[:, 1, :], ALU.subtract))
                elink(stt(blk_f[:, 4, :], blk_f[:, 0, :], float(ROWS // P), blk_f[:, 3, :], ALU.mult, ALU.add))
                elink(stt(blk_f[:, 5, :], blk_f[:, 4, :], float(P), blk_f[:, 2, :], ALU.mult, ALU.mult))
                elink(ts(blk_f[:, 6, :], blk_f[:, 2, :], float(-SPARE), float(SPARE), ALU.mult, ALU.add))
                tt(blk_expert[:, 5:5 + NBLK], blk_f[:, 0, :], blk_f[:, 2, :], ALU.mult)
                tt(blk_row[:, :], blk_f[:, 5, :], blk_f[:, 6, :], ALU.add).then_inc(s_tab, 1)

            def body(b, k):
                na, nf, nk = b + 2, b + 1, 1 - k
                later_weights(dve, b)
                count.clear()

                def full(stage):
                    dve.wait_ge(s_full[BANK[stage]], uses_before(stage, b) + 1)

                def flink(ins, alone=False):
                    link(ins, s_dfront, FRONT_LINKS * na, alone)

                def tlink(ins):
                    link(ins, s_dtail, TAIL_LINKS * (b - 1))

                def mod(j):
                    return mod_in[k][:, j, :].unsqueeze(1)

                for kind, what in stages_of(b):
                    if kind in ("transpose", "scores", "exps"):
                        continue
                    if kind == "normalize":
                        m, u = (b if what < 8 else nf), what % 8
                        dve.wait_ge(s_exps, 8 * m + (u + 1))
                        v.reciprocal(rden[u % 2][:, :], psum_of[u % 2][:, :]).then_inc(s_rden, 1)
                        continue
                    if kind == "max":
                        m = b if what < 8 else nf
                        u = what % 8
                        i, g = QUADS[u]
                        dve.wait_ge(s_scores, 8 * m + (u + 1))
                        for half in range(2):
                            last = v.tensor_reduce(negmax[u % 2][:, half, :],
                                                   scores[u % 2][half][:, :, 0:(i + 1) * P],
                                                   AX_X, ALU.max, negate=True)
                        last.then_inc(s_negmax, 1)
                        continue
                    if kind == "values":
                        i, g = QUADS[what]
                        full(f"pv{what}")
                        last = v.tensor_copy(attnT[k][:, 2 * g:2 * g + 2, i * P:(i + 1) * P],
                                             shared[BANK[f"pv{what}"]][:, 0:2 * P].rearrange("p (a q) -> p a q", a=2))
                        copied(last, f"pv{what}")
                        continue
                    stage = what
                    bank = shared[BANK[stage]] if stage not in NO_BANK else None
                    if stage == "a_stats":
                        if not isinstance(b, int) or b > BODIES[0]:
                            row_statistics(na, k)
                    elif stage == "a_xn":
                        dve.wait_ge(s_rstd, na + 1)
                        norm(xn, lambda i: x_in[k][:, i, :], mv, rstd).then_inc(s_xn, 1)
                    elif stage == "a_va":
                        full(stage)
                        copied(tt(vA[:, :, :], bank[:, 0:NT * D].rearrange("p (i d) -> p i d", i=NT),
                                  bv_bc[:, :].unsqueeze(1).to_broadcast([P, NT, D]), ALU.add), stage)
                    elif stage == "a_sa":
                        full(stage)
                        for i in range(NT):
                            last = v.tensor_reduce(biasA[:, i:i + 1], bank[:, i * P:(2 * i + 1) * P], AX_X,
                                                   ALU.max, negate=True)
                        flink(last)
                        ts(biasA[:, :], biasA[:, :], D ** -0.5, None, ALU.mult).then_inc(s_biasA, 1)
                    elif stage == "a_pva":
                        dve.wait_ge(s_free[BANK["a_sa"]], uses_before("a_sa", b) + 1)
                        flink(v.reciprocal(rsumA[:, :], sumA[:, :]))
                        full(stage)
                        dve.wait_ge(s_mod[k], 8 * na + (16 - 8 * k))
                        for i in range(NT):
                            last = stt(attA[:, i:i + 1, :], bank[:, i * P:(i + 1) * P].unsqueeze(1),
                                       rsumA[:, i:i + 1], mod(GA), ALU.mult, ALU.mult)
                        copied(last, stage)
                    elif stage == "a_x2":
                        dve.wait_ge(s_free[BANK["a_pva"]], uses_before("a_pva", b) + 1)
                        ins = tt(base_all[:, span(2 * na, NT), :], attA[:, :, :], x_in[k][:, :, :], ALU.add)
                        ins.then_inc(s_x2, 1)
                        wait_alone(dve, s_x2, na + 1, CONSTS)
                        for i in range(NT):
                            last = v.bn_stats(stats2[:, i, :], base_all[:, span(2 * na + i, 1), :])
                        flink(last, alone=True)
                        for i in range(NT):
                            last = v.bn_aggr(mv2[:, i, :], stats2[:, i, :])
                        last.then_inc(s_var2, 1)
                    elif stage == "a_ln2":
                        dve.wait_ge(s_rstd2, na + 1)
                        for i in range(NT):
                            last = stt(xn2[:, i:i + 1, :], base_all[:, span(2 * na + i, 1), :], mv2[:, i, 0:1],
                                       mod(CB), ALU.subtract, ALU.mult)
                        flink(last)
                        for i in range(NT):
                            last = stt(h2[:, span(2 * na + i, 1), :], xn2[:, i:i + 1, :], rstd2[:, i:i + 1],
                                       mod(SB), ALU.mult, ALU.add)
                        last.then_inc(s_h2, 1)
                    elif stage == "a_sq":
                        dve.wait_ge(s_h2, na + 1)
                        for i in range(NT):
                            rows = h2[:, span(2 * na + i, 1), :]
                            last = stt(squares[:, i:i + 1, :], rows, 1.0, rows, ALU.mult, ALU.mult,
                                       accum_out=ms2[:, i:i + 1])
                        last.then_inc(s_ms2, 1)
                    elif stage == "t_sq":
                        dve.wait_ge(s_free[BANK["t_wo1"]], uses_before("t_wo1", b) + 1)
                        for i in range(NT):
                            last = stt(squares3[:, i, :], h[:, i, :], 1.0, h[:, i, :], ALU.mult, ALU.mult,
                                       accum_out=ms3[:, i:i + 1])
                        last.then_inc(s_ms3, 1)
                    elif stage == "a_xr":
                        dve.wait_ge(s_rms2, na + 1)
                        dve.wait_ge(s_h2, na + 1)
                        for i in range(NT):
                            last = ts(xr[:, i:i + 1, :], h2[:, span(2 * na + i, 1), :], rms2[:, i:i + 1], None, ALU.mult)
                        last.then_inc(s_xr, 1)
                    elif stage.startswith("f_p"):
                        i, j = int(stage[3]), "kab".index(stage[4])
                        m = 3 * i + j
                        heads = HKV if j == 0 else 8
                        tab = 2 if j == 0 else 0
                        full(stage)
                        wait(dve, s_roped, 6 * nf + (m - 1))
                        if j == 0:
                            v.tensor_copy(vtok[nk][:, i, :, :], bank[:, HKV * K:].rearrange(
                                "p (h d) -> p h d", h=HKV)).then_inc(s_vtok, 1)
                        q = bank[:, 0:heads * K].rearrange("p (h d) -> p h d", h=heads)
                        cos, sin = (r[m % 2][:, 0:heads * K].rearrange("p (h d) -> p h d", h=heads)
                                    for r in (rope_cos, rope_sin))

                        def table(w, lo, hi):
                            return rope[:, tab + w, i, lo:hi].unsqueeze(1).to_broadcast([P, heads, hi - lo])

                        tt(cos, q, table(0, 0, K), ALU.mult)
                        tt(sin[:, :, 0:K // 2], q[:, :, K // 2:K], table(1, 0, K // 2), ALU.mult)
                        last = tt(sin[:, :, K // 2:K], q[:, :, 0:K // 2], table(1, K // 2, K), ALU.mult)
                        copied(last, stage)
                    elif stage in ("t_wo0", "t_wo1"):
                        i = int(stage[4])
                        full(stage)
                        copied(tt(h[:, i:i + 1, :], bank[:, 0:D].unsqueeze(1), h2[:, span(2 * b - 2 + i, 1), :],
                                  ALU.add), stage)
                    elif stage == "t_xf":
                        dve.wait_ge(s_rms3, b)
                        dve.wait_ge(s_free[BANK["t_wo1"]], uses_before("t_wo1", b) + 1)
                        wait(dve, s_scat, 16 * NT * (b - 1))
                        for i in range(NT):
                            stt(xf[:, i, 0:D], h[:, i, :], rms3[:, i:i + 1], g2_bc[:, :], ALU.mult, ALU.mult)
                        last = v.tensor_copy(xf[:, :, D:D + 1], small[:, span(2 * b + (C_TOKEN - 2), NT)].unsqueeze(2))
                        last.then_inc(s_xf, 1)
                    elif stage == "t_logits":
                        full(stage)
                        last = tt(logits[:, :, :], bank[:, 0:NT * E].rearrange("p (i e) -> p i e", i=NT),
                                  rb_bc[:, :].unsqueeze(1).to_broadcast([P, NT, E]), ALU.add)
                        copied(last, stage)
                    elif stage == "t_top":
                        wait_alone(dve, s_free[BANK["t_logits"]], uses_before("t_logits", b) + 1, CONSTS)
                        for i in range(NT):
                            last = v.max(top8[:, i, :], logits[:, i, :])
                        tlink(last)
                        tt(gap[:, :], top8[:, :, 1], top8[:, :, 0], ALU.subtract).then_inc(s_gap, 1)
                        for i in range(NT):
                            last = v.max_index(idx8[:, i, :], top8[:, i, :], logits[:, i, :])
                        tlink(last)
                        tlink(v.tensor_copy(idxf[:, :, :], idx8[:, :, 0:2]))
                        ik = "p i k e -> p (i k) e"
                        tlink(tt(picked[:, :, :, :].rearrange(ik), iota8.unsqueeze(1).to_broadcast([P, NT * 2, E]),
                                 idxf[:, :, :].rearrange("p i k -> p (i k)").unsqueeze(2)
                                 .to_broadcast([P, NT * 2, E]), ALU.is_equal))
                        v.tensor_copy(picked_bf[:, :, 0, :], picked[:, :, 0, :])
                        tt(picked_bf[:, :, 1, :], picked[:, :, 0, :], picked[:, :, 1, :], ALU.add
                           ).then_inc(s_picked, 1)
                    elif stage == "t_cum":
                        full(stage)
                        last = stt(kept[:, :, :, :].rearrange("p i k e -> p (i k e)"), bank[:, 0:NT * 2 * E],
                                   float(CAP), picked[:, :, :, :].rearrange("p i k e -> p (i k e)"),
                                   ALU.is_lt, ALU.mult)
                        copied(last, stage)
                    elif stage == "t_keep":
                        dve.wait_ge(s_free[BANK["t_cum"]], uses_before("t_cum", b) + 1)
                        tlink(tt(seen_bf[:, :, :], seen_bf[:, :, :], picked_bf[:, 0], ALU.add))
                        tlink(tt(seen_bf[:, :, :], seen_bf[:, :, :], picked_bf[:, 1], ALU.add))
                        ik = "p i k e -> p (i k) e"
                        v.tensor_reduce(kept_any[:, :, :].rearrange("p i k -> p (i k)"),
                                        kept[:, :, :, :].rearrange(ik), AX_X, ALU.add)
                        tlink(tt(kept_id[:, :, :, :].rearrange(ik), kept[:, :, :, :].rearrange(ik),
                                 iota8.unsqueeze(1).to_broadcast([P, NT * 2, E]), ALU.mult))
                        tlink(v.tensor_reduce(kept_expert[:, :, :].rearrange("p i k -> p (i k)"),
                                              kept_id[:, :, :, :].rearrange(ik), AX_X, ALU.add))
                        tt(has[:, :], kept_any[:, :, 0], kept_any[:, :, 1], ALU.max)
                        tlink(tt(expert[:, :], kept_expert[:, :, 0], kept_expert[:, :, 1], ALU.max))
                        tlink(tt(mine[:, :, :], iota8.unsqueeze(1).to_broadcast([P, NT, E]),
                                 expert[:, :].unsqueeze(2).to_broadcast([P, NT, E]), ALU.is_equal))
                        tt(mine_bf[:, :, :], mine[:, :, :], has[:, :].unsqueeze(2).to_broadcast([P, NT, E]),
                           ALU.mult).then_inc(s_mine, 1)
                    elif stage == "t_score":
                        dve.wait_ge(s_gexp, b)
                        tlink(ts(gap_den[:, :], gap_exp[:, :], 1.0, None, ALU.add))
                        tlink(v.reciprocal(score[:, :, 0], gap_den[:, :]))
                        tlink(tt(score[:, :, 1], score[:, :, 0], gap_exp[:, :], ALU.mult))
                        tlink(tt(kept_score[:, :, :], kept_any[:, :, :], score[:, :, :], ALU.mult))
                        v.tensor_reduce(xf[:, :, D + 1], kept_score[:, :, :], AX_X, ALU.add).then_inc(s_score, 1)
                        tlink(tt(score[:, :, :], score[:, :, :], kept_score[:, :, :], ALU.subtract))
                        tlink(v.tensor_reduce(drop_score[:, :], score[:, :, :], AX_X, ALU.add))
                    elif stage == "t_rank":
                        full(stage)
                        last = tt(rank_of[:, :, :], bank[:, 0:NT * E].rearrange("p (i e) -> p i e", i=NT),
                                  mine_bf[:, :, :], ALU.mult)
                        copied(last, stage)
                    elif stage == "t_row":
                        dve.wait_ge(s_free[BANK["t_rank"]], uses_before("t_rank", b) + 1)
                        tlink(tt(filled_bf[:, :], filled_bf[:, :], mine_bf[:, 0, :], ALU.add))
                        tt(filled_bf[:, :], filled_bf[:, :], mine_bf[:, 1, :], ALU.add).then_inc(s_filled, 1)
                        tlink(v.tensor_reduce(rank[:, :], rank_of[:, :, :], AX_X, ALU.add))
                        tlink(stt(row[:, :], expert[:, :], float(ROWS), rank[:, :], ALU.mult, ALU.add))
                        ts(dump_row[:, :], has[:, :], -1.0, 1.0, ALU.mult, ALU.add)
                        tlink(stt(row[:, :], row[:, :], -1.0, has[:, :], ALU.add, ALU.mult))
                        tlink(tt(dump_row[:, :], dump_row[:, :], small[:, span(2 * b + (C_DUMP - 2), NT)], ALU.mult))
                        tt(scatter_idx[:, :], row[:, :], dump_row[:, :], ALU.add).then_inc(s_sidx, 1)
                        if isinstance(b, int) and b == NBATCH:
                            block_table()
                    elif stage == "t_base":
                        if isinstance(b, int) and b == 1:
                            dve.wait_ge(s_gb, 16)
                        for i in range(NT):
                            last = stt(base_tmp[:, i, :], xf[:, i, 0:D], drop_score[:, i:i + 1], h[:, i, :],
                                       ALU.mult, ALU.add)
                        tlink(last)
                        tlink(tt(base_tmp[:, :, :], base_tmp[:, :, :],
                                 gb_all[:, span(b - 1, 1), :].to_broadcast([P, NT, D]), ALU.mult))
                        rows = base_all[:, span(2 * b - 2, NT), :]
                        tlink(tt(rows, rows, base_tmp[:, :, :], ALU.add))
                for s_, size in ((s_dfront, FRONT_LINKS), (s_dtail, TAIL_LINKS),
                                 (s_dstats, STATS_LINKS)):
                    assert count.get(id(s_), size) == size, (part, count[id(s_)], size)

            bodies(dve, body)

            def step(t, k):
                if has_block(t, 0):
                    dve.wait_ge(s_xb[k], 16 // XBUFS * t + (16 - 16 // XBUFS * k))
                    number = xb[k][:, D:D + 1]
                    stt(past[:, span(t, 1)], number, 0.0, small[:, span(t + C_PAST, 1)], ALU.is_equal, ALU.mult
                        ).then_inc(s_past, 1)
                    dve.wait_ge(s_past, t + 1)
                    v.tensor_copy(row_score[:, span(t, 1)], xb[k][:, D + 1:D + 2])
                    stt(result_row[:, span(t, 1)], past[:, span(t, 1)], -1.0, number, ALU.add, ALU.add
                        ).then_inc(s_token, 1)
                if has_block(t, 2):
                    j, m = t - 2, k % 2
                    dve.wait_ge(s_upc, j + 1)
                    wait(dve, s_hid, j - 1)
                    tt(prod[m], scores[1][m][:, 1, :], up[m], ALU.mult).then_inc(s_prod, 1)
                if has_block(t, 6):
                    j, m = t - 6, (k - 6) % YBUFS
                    dve.wait_ge(s_yp, j + 1)
                    if not isinstance(j, int) or j >= YBUFS:
                        dve.wait_ge(s_ys[m], 16 // YBUFS * j - 16 // YBUFS * m)
                    ts(yb[m], shared[m % 2][:, 0:D], row_score[:, span(j, 1)], None, ALU.mult).then_inc(s_yb, 1)
                if has_block(t, 4):
                    j, m = t - 4, k % 2
                    dve.wait_ge(s_hTp, j + 1)
                    wait(dve, s_yp, j - 1)
                    v.tensor_copy(hidT[m], tposed[m][:, 0:HID]).then_inc(s_hT, 1)

            steps(dve, step)

            finish(dve, v, [m for m in range(NBATCH // OUTS) if m not in POOL_OUTS])


_INS = ["L0_attn_x", "L0_attn_W", "L0_attn_b", "L0_ffn_g1", "L0_ffn_g2", "L0_ffn_wq", "L0_ffn_wk", "L0_ffn_wv",
        "L0_ffn_wo", "L0_ffn_router_w", "L0_ffn_router_b", "L0_ffn_w1", "L0_ffn_w2", "L0_ffn_w3", "L0_c",
        "L0_wmod"]


def shape_constants():
    f32 = np.float32
    rows = np.arange(P)
    ident = np.eye(P, dtype=f32)
    mask = np.where(rows[None, :] > rows[:, None], f32(MASKED), f32(0)).astype(f32)
    upper = (rows[:, None] <= rows[None, :]).astype(f32)
    thetas = 10000.0 ** (-np.arange(0, K, 2, dtype=f32) / K)
    ticks = np.tile(np.outer(np.arange(T, dtype=f32), thetas), (1, 2))
    cos = np.cos(ticks).astype(f32)
    sin = np.sin(ticks).astype(f32)
    sin[:, :K // 2] *= -1
    scale = f32(K ** -0.5)
    tables = np.stack([cos * scale, sin * scale, cos, sin])
    rope = np.ascontiguousarray(tables.reshape(4, NT, P, K).transpose(2, 0, 1, 3))
    small = np.zeros((P, C_END), f32)
    small[:, C_IOTA8:C_IOTA8 + E] = np.arange(E)
    small[:, C_DUMP:C_DUMP + NBATCH * NT] = DUMP + P * np.arange(NBATCH * NT)[None, :] + rows[:, None]
    small[:, C_THR:C_THR + E * E] = np.tile(P * np.arange(E), E)
    small[:, C_LOWER:C_LOWER + E * E] = np.tril(np.ones((E, E))).ravel()
    small[:, C_BLK:C_BLK + NBLK] = np.arange(NBLK)
    small[:, C_HALF:C_HALF + 2] = -0.5
    small[:, C_TOKEN:C_PAST] = 1 + P * np.arange(NBATCH * NT)[None, :] + rows[:, None]
    small[:, C_PAST:C_END] = 1 + NTOK + P * np.arange(NBLK)[None, :] + rows[:, None]
    return {"k_ident": ident, "k_mask": mask, "k_upper": upper, "k_rope": rope, "k_small": small}


def kernel(**inputs):
    import numpy as _np
    import concourse.bacc as _bacc
    from concourse import mybir as _mybir
    from concourse.bass_utils import run_bass_kernel_spmd as _run

    nc = _bacc.Bacc("TRN2", target_bir_lowering=False, num_devices=1)
    arrays, args = {}, []
    for name, a in [(n, inputs[n]) for n in _INS] + list(shape_constants().items()):
        a = _np.ascontiguousarray(a)
        arrays[f"in_{name}"] = a
        args.append(nc.dram_tensor(f"in_{name}", a.shape, _mybir.dt.from_np(a.dtype), kind="ExternalInput").ap())
    args.append(nc.dram_tensor("out_dram", (NBATCH, T, D), F32, kind="ExternalOutput").ap())
    adaln_layer(nc, *args)
    r = _run(nc, [arrays], core_ids=[0])
    return r.results[0]["out_dram"]
```
